# Optimizing a Trainium2 kernel written in Bass

```python
import numpy as np
import jax
import jax.numpy as jnp

def _softmax(x, axis=-1):
    return jax.nn.softmax(x, axis=axis)

def _gelu(x):
    return jax.nn.gelu(x, approximate=True)

def _silu(x):
    return jax.nn.silu(x)

def _sigmoid(x):
    return jax.nn.sigmoid(x)

def _layernorm(x, axis=-1, eps=1e-05):
    m = jnp.mean(x, axis=axis, keepdims=True)
    v = jnp.var(x, axis=axis, keepdims=True)
    return (x - m) / jnp.sqrt(v + eps)

def _scatter_add(tgt, idx, src, axis=0):
    return tgt.at[idx].add(src)

def _segment_sum(src, seg, n):
    return jax.ops.segment_sum(src, seg, n)
kernel_name = 'mk_recurrent_d1_jaxref_r8_c84225'

def setup_inputs(seed: int=0):
    np.random.seed(seed)
    _w = jnp.asarray

    def _L0_attn_setup():
        import jax, jax.numpy as jnp
        import numpy as np
        H = 16
        EPS = 1e-12

        def _l2norm(t):
            n = jnp.sqrt(jnp.sum(t * t, axis=-1, keepdims=True))
            return t / jnp.maximum(n, EPS)
        key = jax.random.key(seed)
        ks = jax.random.split(key, 7)
        B, L, D = (2, 256, 128)
        s = 0.02
        return {'x': jax.random.normal(ks[0], (B, L, D), dtype=jnp.float32), 'Wq': jax.random.normal(ks[1], (D, D), dtype=jnp.float32) * s, 'Wk': jax.random.normal(ks[2], (D, D), dtype=jnp.float32) * s, 'Wv': jax.random.normal(ks[3], (D, D), dtype=jnp.float32) * s, 'Wo': jax.random.normal(ks[4], (D, D), dtype=jnp.float32) * s, 'Wb': jax.random.normal(ks[5], (D, H), dtype=jnp.float32) * s, 'bb': jnp.zeros((H,), dtype=jnp.float32)}
    _L0_attn_in = _L0_attn_setup()

    def _L0_ffn_setup():
        import jax, jax.numpy as jnp
        import numpy as np
        B, S, D, F, E = (8, 128, 128, 512, 8)
        EPS = 1e-05
        key = jax.random.key(seed)
        ks = jax.random.split(key, 4)
        s = 0.02
        return {'input_features': jax.random.normal(ks[0], (B, S, D), jnp.float32), 'centroids': jax.random.normal(ks[1], (E, D), jnp.float32) * 0.1, 'ln_g': jnp.ones((E, D), jnp.float32), 'ln_b': jnp.zeros((E, D), jnp.float32), 'w1': jax.random.normal(ks[2], (E, D, F), jnp.float32) * s, 'b1': jnp.zeros((E, F), jnp.float32), 'w2': jax.random.normal(ks[3], (E, F, D), jnp.float32) * s, 'b2': jnp.zeros((E, D), jnp.float32)}
    _L0_ffn_in = _L0_ffn_setup()
    _d = {'L0_attn_x': _L0_attn_in['x'], 'L0_attn_Wq': _L0_attn_in['Wq'], 'L0_attn_Wk': _L0_attn_in['Wk'], 'L0_attn_Wv': _L0_attn_in['Wv'], 'L0_attn_Wo': _L0_attn_in['Wo'], 'L0_attn_Wb': _L0_attn_in['Wb'], 'L0_attn_bb': _L0_attn_in['bb'], 'L0_ffn_centroids': _L0_ffn_in['centroids'], 'L0_ffn_ln_g': _L0_ffn_in['ln_g'], 'L0_ffn_ln_b': _L0_ffn_in['ln_b'], 'L0_ffn_w1': _L0_ffn_in['w1'], 'L0_ffn_b1': _L0_ffn_in['b1'], 'L0_ffn_w2': _L0_ffn_in['w2'], 'L0_ffn_b2': _L0_ffn_in['b2']}
    _x0 = _d['L0_attn_x']
    _d['L0_attn_x'] = jax.random.normal(jax.random.fold_in(jax.random.key(seed), 1), (8, 512, 128), dtype=_x0.dtype)
    del _x0
    return _d

def reference(L0_attn_x, L0_attn_Wq, L0_attn_Wk, L0_attn_Wv, L0_attn_Wo, L0_attn_Wb, L0_attn_bb, L0_ffn_centroids, L0_ffn_ln_g, L0_ffn_ln_b, L0_ffn_w1, L0_ffn_b1, L0_ffn_w2, L0_ffn_b2):

    def _L0_attn_ref(x, Wq, Wk, Wv, Wo, Wb, bb):
        import jax, jax.numpy as jnp
        import numpy as np
        H = 16
        EPS = 1e-12

        def _l2norm(t):
            n = jnp.sqrt(jnp.sum(t * t, axis=-1, keepdims=True))
            return t / jnp.maximum(n, EPS)
        B, L, Dm = x.shape
        Dh = Dm // H
        q = (x @ Wq).reshape(B, L, H, Dh)
        k = (x @ Wk).reshape(B, L, H, Dh)
        v = (x @ Wv).reshape(B, L, H, Dh)
        beta = jax.nn.sigmoid(x @ Wb + bb)
        q = _l2norm(q)
        k = _l2norm(k)
        scores = jnp.einsum('blhd,bthd->bhlt', q, k)
        scores = scores * beta.transpose(0, 2, 1)[:, :, None, :]
        mask = jnp.tril(jnp.ones((L, L), dtype=scores.dtype))
        scores = scores * mask
        out = jnp.einsum('bhlt,bthe->blhe', scores, v).reshape(B, L, Dm)
        return out @ Wo

    def _L0_ffn_ref(input_features, centroids, ln_g, ln_b, w1, b1, w2, b2):
        import jax, jax.numpy as jnp
        import numpy as np
        B, S, D, F, E = (8, 128, 128, 512, 8)
        EPS = 1e-05
        x = input_features.reshape(-1, D)
        aff = jax.lax.stop_gradient(x @ centroids.T)
        eid = jnp.argmax(aff, axis=-1)
        alpha = jax.nn.sigmoid(jnp.sum(x * centroids[eid], axis=-1, keepdims=True))
        mu = jnp.mean(x, axis=-1, keepdims=True)
        var = jnp.mean((x - mu) ** 2, axis=-1, keepdims=True)
        xn = (x - mu) * jax.lax.rsqrt(var + EPS)
        xln = xn * ln_g[eid] + ln_b[eid]
        onehot = jax.nn.one_hot(eid, E, dtype=x.dtype)
        ffn = jnp.zeros_like(x)
        for e in range(E):
            h = jax.nn.relu(xln @ w1[e] + b1[e])
            ffn = ffn + onehot[:, e:e + 1] * (h @ w2[e] + b2[e])
        out = x + alpha * ffn
        return out.reshape(input_features.shape)
    x = L0_attn_x
    xn = _layernorm(x, axis=-1)
    s = _L0_attn_ref(xn, L0_attn_Wq, L0_attn_Wk, L0_attn_Wv, L0_attn_Wo, L0_attn_Wb, L0_attn_bb)
    g = _silu(_L0_ffn_ref(xn, L0_ffn_centroids, L0_ffn_ln_g, L0_ffn_ln_b, L0_ffn_w1, L0_ffn_b1, L0_ffn_w2, L0_ffn_b2))
    x = x + s * g
    return x

_drawn_inputs = setup_inputs


def setup_inputs(seed=0):
    import zlib

    import numpy as np

    out = dict(_drawn_inputs(seed))
    spreads = {'L0_attn_bb': (0.0, 0.746),
     'L0_ffn_ln_g': (1.0, 0.6),
     'L0_ffn_ln_b': (0.0, 0.8),
     'L0_ffn_b1': (0.0, 0.8),
     'L0_ffn_b2': (0.0, 0.586)}
    factors = {'L0_attn_Wb': 5.661, 'L0_ffn_centroids': 3.4, 'L0_ffn_w1': 6.354, 'L0_ffn_w2': 4.988}
    for name, (base, spread) in spreads.items():
        noise = np.random.default_rng([zlib.crc32(name.encode()), seed]).standard_normal(out[name].shape)
        drawn = base * np.exp(spread * noise) if base else spread * noise
        out[name] = jnp.asarray(drawn.astype(out[name].dtype))
    for name, factor in factors.items():
        out[name] = (out[name] * factor).astype(out[name].dtype)
    return out
```

```python
from contextlib import ExitStack

import concourse.bass as bass
from concourse import mybir

F32 = mybir.dt.float32
BF16 = mybir.dt.bfloat16
I32 = mybir.dt.int32
ALU = mybir.AluOpType
ACT = mybir.ActivationFunctionType
AX = mybir.AxisListType

P = 128
D = 128
H, DH = 16, 8
SEQS, SEQ = 8, 512
NT = SEQS * SEQ // P
TPS = SEQ // P
E, F = 8, 512
FC = F // P
TOKENS = NT * P
SLOTS = NT + E - 1
KVW = DH * H * DH
CQ, CK, CV, CB, CA = 0, D, 2 * D, 3 * D, 3 * D + H
PW = CA + E
RN, RX, RS, RALPHA, RMEAN, RRSTD = 0, D, 2 * D, 3 * D, 3 * D + 1, 3 * D + 2
RW = 3 * D + 3
LN_EPS = 1e-5
NORM_EPS2 = 1e-24
NOWHERE = 8192.0
PAD = 16
RB = 3
RG = 9
AHEAD = SLOTS + 1
FIRST = 3


def build(nc, x, wq, wk, wv, wo, wb, bb, cent, ln_g, ln_b, w1, b1, w2, b2, out):
    rows_dram = nc.dram_tensor("token_rows", (TOKENS, RW), F32).ap()
    xt = x.rearrange("s (j p) d -> p (s j) d", p=P)
    out_rows = out.rearrange("s l d -> (s l) d")
    ctx = ExitStack()
    with ctx:
        def sb(name, shape, dt=F32):
            return ctx.enter_context(nc.sbuf_tensor(name, shape, dt))

        def ps(name, shape, dt=F32):
            return ctx.enter_context(nc.psum_tensor(name, shape, dt))

        def sem(name):
            return ctx.enter_context(nc.semaphore(name))

        row = sb("row", [P, NT, RW])
        proj = sb("proj", [P, NT, PW])
        wcat = sb("wcat", [D, PW])
        wo_sb = sb("wo_sb", [D, D])
        small = sb("small", [3 * E, D])
        gb = sb("gb", [D, 2 * E])
        bb_bc = sb("bb_bc", [P, H])
        w1_sb = sb("w1_sb", [D, E, F])
        w2_sb = sb("w2_sb", [P, E, FC, D])
        b1_bc = sb("b1_bc", [P, E, F])
        b2_bc = sb("b2_bc", [P, E, D])
        col = sb("col", [P, D])
        colhead = sb("colhead", [P, H, DH])
        pidx = sb("pidx", [P, 1])
        pidx_i = sb("pidx_i", [P, 1], I32)
        phead_i = sb("phead_i", [P, 1], I32)
        phead = sb("phead", [P, 1])
        rev = sb("rev", [P, E])
        steps = sb("steps", [P, NT])
        tileno = sb("tileno", [P, NT])
        slotno = sb("slotno", [P, AHEAD])
        ident = sb("ident", [P, P])
        tri = sb("tri", [P, P])
        before = sb("before", [P, P], BF16)
        ones = sb("ones", [P, P], BF16)
        same_head = sb("same_head", [P, P])
        st1 = sb("st1", [P, TPS, 6])
        mean1 = sb("mean1", [P, TPS])
        var1 = sb("var1", [P, TPS])
        dif1 = sb("dif1", [P, TPS])
        rs1 = sb("rs1", [P, TPS])
        nt1 = sb("nt1", [P, TPS])
        rs2 = sb("rs2", [P, NT])
        nt2 = sb("nt2", [P, NT])
        st2 = sb("st2", [P, NT, 6])
        xs = sb("xs", [P, TPS, D])
        qk = xs[:, :, :].rearrange("p (i a) c -> p i (a c)", i=2)
        xT = sb("xT", [D, 2, P])
        m = sb("m", [P, KVW])
        sq = m[:, :].rearrange("p (j c) -> p j c", j=TPS)
        rnorm = sb("rnorm", [P, NT, 2 * H])
        work = sb("work", [P, RB * (2 * F + 5 * D)])
        used = [0]

        def part(words):
            used[0] += words
            assert used[0] <= RB * (2 * F + 5 * D)
            return work[:, used[0] - words:used[0]]

        logit = part(NT * H).rearrange("p (n h) -> p n h", n=NT)
        mx = sb("mx", [P, NT])
        eq = part(NT * E).rearrange("p (n e) -> p n e", n=NT)
        mw = sb("mw", [P, NT])
        oh = sb("oh", [P, NT, E], BF16)
        PREW = (PAD + NT) * E
        pre = [m[:, i * PREW:i * PREW + PREW].rearrange("p (n e) -> p n e", e=E) for i in range(2)]
        cmp = part(NT * E).rearrange("p (e n) -> p e n", e=E)
        pe8 = [sb(f"pe8{i}", [P, 4 + E]) for i in range(2)]
        pos = sb("pos", [P, NT])
        pos_i = sb("pos_i", [P, NT], I32)
        pa_i = sb("pa_i", [P, NT], I32)
        pb_i = sb("pb_i", [P, NT], I32)
        pa = sb("pa", [P, NT])
        pb = sb("pb", [P, NT])
        ohb = part(NT * P // 2).bitcast(BF16).rearrange("p (n c) -> p n c", n=NT)
        oha = part(NT * 3 * AHEAD // 2).bitcast(BF16).rearrange("p (n a s) -> p n a s", n=NT, a=3)
        inv = sb("inv", [P, 3, AHEAD])
        tok = sb("tok", [P, AHEAD])
        past = sb("past", [P, AHEAD])
        gidx = sb("gidx", [P, AHEAD], I32)
        sidx = sb("sidx", [P, AHEAD], I32)
        scmp = sb("scmp", [1, AHEAD, E - 1])
        sexp = sb("sexp", [1, AHEAD])
        sexp_i = sb("sexp_i", [1, AHEAD], I32)
        kv = sb("kv", [P, 2, KVW])
        attn = sb("attn", [P, 2, D])
        state = sb("state", [P, 2, D])
        qT = sb("qT", [P, 2, P])
        aT = xT
        rn = rnorm[:, :, :].rearrange("p n c -> p (n c)")
        rn_sqrt = kv[:, 0, :]
        rg = proj
        used[0] = 0
        xl, xlT, y, sg, o = (part(RB * D).rearrange("p (r c) -> p r c", r=RB) for _ in range(5))
        h = part(RB * F).rearrange("p (r f) -> p r f", r=RB)
        hT = part(RB * F).rearrange("p (r c t) -> p r c t", r=RB, c=FC)

        bank = ps("bank", [P, 8, 512])
        prefix = bank[:, 0:4, :].rearrange("p (i a) c -> p i (a c)", i=2)
        small_ps = bank[:, 6, 0:3 * E]
        sum_ps = bank[:, 6, :]
        inv_ps = bank[:, 7, 0:3 * AHEAD]
        st_ps = bank[:, 4, 0:D]
        T_ps = bank[:, 5, 0:P]
        in_ps = bank[:, 6, 0:D]
        s_ps = bank[:, 7, 0:D]
        h_ps = [bank[:, i, :] for i in (0, 1, 2)]
        hT_ps = [bank[:, i, :] for i in (3, 4, 6)]
        y_ps = bank[:, 7, 0:D]

        (x_in, w_in, small_in, wo_in, ffn_in, iota_ok, const_ok, head_ok, small_T, small_ok,
         st1_ok, ag1_ok, ag1b_ok, rs1_ok, xn_ok, st2_ok, rs2_ok, xT_ps_ok, xT_ok, pj_ps_ok, pj_ok, sq_ok,
         ss_ok, xrow_ok, qk_ok, rn_ok, qn_ok, va_ok, vr_ok, na_ok, nb_ok, va2_ok, rs2_all, ss_all, ss_sqrt, logit_ok, sig_ok, bvs_ok, mx_ok, alpha_ok, dv,
         oh_ok, rank_ok, oneh_ok, inv_ok, idx_ok,
         bv_ok, kv_ok, pre_ok, m_ok, red_ok, qT_ps_ok, qT_ok, st_ps_ok, st_ok, inter_ok, attn_ok,
         aT_ps_ok, aT_ok, s_ps_ok, s_ok, rows_out,
         xl_ok, xlT_ps_ok, xlT_ok, h_ps_ok, h_ok, hT_ps_ok, hT_ok, y_ps_ok,
         y1_ok, y2_ok, sg_ok, y3_ok, y4_ok, o_ok, o_free) = (sem(n) for n in (
             "x_in", "w_in", "small_in", "wo_in", "ffn_in", "iota_ok", "const_ok", "head_ok", "small_T", "small_ok",
             "st1_ok", "ag1_ok", "ag1b_ok", "rs1_ok", "xn_ok", "st2_ok", "rs2_ok", "xT_ps_ok", "xT_ok", "pj_ps_ok",
             "pj_ok", "sq_ok",
             "ss_ok", "xrow_ok", "qk_ok", "rn_ok", "qn_ok", "va_ok", "vr_ok", "na_ok", "nb_ok", "va2_ok", "rs2_all", "ss_all", "ss_sqrt", "logit_ok", "sig_ok", "bvs_ok", "mx_ok", "alpha_ok", "dv",
             "oh_ok", "rank_ok", "oneh_ok", "inv_ok", "idx_ok",
             "bv_ok", "kv_ok", "pre_ok", "m_ok", "red_ok", "qT_ps_ok", "qT_ok", "st_ps_ok", "st_ok", "inter_ok",
             "attn_ok", "aT_ps_ok", "aT_ok", "s_ps_ok", "s_ok", "rows_out",
             "xl_ok", "xlT_ps_ok", "xlT_ok", "h_ps_ok", "h_ok", "hT_ps_ok", "hT_ok", "y_ps_ok",
             "y1_ok", "y2_ok", "sg_ok", "y3_ok", "y4_ok", "o_ok", "o_free"))
        gath = [sem(f"gath{i}") for i in range(RG)]
        scat = [sem(f"scat{i}") for i in range(RB)]

        def slot_steps(eng, step):
            for s in range(FIRST):
                step(s, s)
            with eng.Fori(0, (SLOTS - FIRST) // RG) as it:
                for k in range(FIRST, FIRST + RG):
                    step(it * RG + k, k)
            for s in range(SLOTS, SLOTS + FIRST):
                step(s, s)

        def real(s):
            return not isinstance(s, int) or 0 <= s < SLOTS

        block = ctx.enter_context(nc.Block())

        @block.sync
        def _(sp):
            sp.dma_start(row[:, :, RX:RX + D], xt).then_inc(x_in, 16)
            sp.dma_start(wo_sb[:, :], wo).then_inc(wo_in, 16)
            sp.dma_start(w1_sb[:, :, :], w1.rearrange("e d f -> d e f")).then_inc(ffn_in, 16)
            sp.dma_start(w2_sb[:, :, :, :], w2.rearrange("e (c p) d -> p e c d", p=P)).then_inc(ffn_in, 16)
            sp.dma_start(b1_bc[:, :, :], b1.partition_broadcast(P)).then_inc(ffn_in, 16)
            sp.dma_start(b2_bc[:, :, :], b2.partition_broadcast(P)).then_inc(ffn_in, 16)
            sp.wait_ge(alpha_ok, 1)
            sp.wait_ge(xrow_ok, SEQS)
            sp.wait_ge(rs2_all, 1)
            with sp.Fori(0, SEQS) as b:
                sp.wait_ge(s_ok, b * TPS + TPS)
                sp.dma_start(rows_dram[bass.ds(b * SEQ, SEQ), :].rearrange("(j p) c -> p j c", p=P),
                             row[:, bass.ds(b * TPS, TPS), :]).then_inc(rows_out, 16)

        @block.gpsimd
        def _(pool):
            g = nc.gpsimd
            g.iota(col[:, :], [[1, D]], base=0, channel_multiplier=0,
                   allow_small_or_imprecise_dtypes=True)
            g.iota(colhead[:, :, :], [[1, H], [0, DH]], base=0, channel_multiplier=0,
                   allow_small_or_imprecise_dtypes=True)
            g.iota(pidx[:, :], [[0, 1]], base=0, channel_multiplier=1,
                   allow_small_or_imprecise_dtypes=True)
            g.iota(pidx_i[:, :], [[0, 1]], base=0, channel_multiplier=1)
            g.iota(rev[:, :], [[-1, E]], base=E, channel_multiplier=0,
                   allow_small_or_imprecise_dtypes=True)
            g.iota(steps[:, :], [[P, NT]], base=0, channel_multiplier=0,
                   allow_small_or_imprecise_dtypes=True)
            g.iota(tileno[:, :], [[1, NT]], base=0, channel_multiplier=0,
                   allow_small_or_imprecise_dtypes=True)
            g.iota(slotno[:, :], [[1, AHEAD]], base=0, channel_multiplier=0,
                   allow_small_or_imprecise_dtypes=True).then_inc(iota_ok, 1)

            with pool.Fori(0, SEQS) as b:
                pool.wait_ge(xn_ok, b + 1)
                g.tensor_copy(row[:, bass.ds(b * TPS, TPS), RN:RN + D], xs[:, :, :]).then_inc(xrow_ok, 1)

            pool.wait_ge(bvs_ok, 1)
            with pool.Fori(0, SEQS) as b:
                v4 = proj[:, bass.ds(b * TPS, TPS), CV:CV + D].rearrange("p j (h e) -> p j h e", e=DH)
                s4 = rnorm[:, bass.ds(b * TPS, TPS), H:2 * H].unsqueeze(3).to_broadcast([P, TPS, H, DH])
                g.tensor_tensor(v4, v4, s4, ALU.mult).then_inc(bv_ok, 1)
                pool.wait_ge(bv_ok, b + 1)
                for j in range(TPS):
                    n = b * TPS + j
                    pool.wait_ge(pre_ok, n + 1)
                    k3 = proj[:, bass.ds(n, 1), CK:CK + D].rearrange("p o (h d) -> p (o d) h", d=DH)
                    v3 = proj[:, bass.ds(n, 1), CV:CV + D].rearrange("p o (h e) -> p (o h) e", e=DH)
                    g.tensor_tensor(kv[:, j % 2, :].rearrange("p (d h e) -> p d h e", d=DH, h=H),
                                    k3.unsqueeze(3).to_broadcast([P, DH, H, DH]),
                                    v3.unsqueeze(1).to_broadcast([P, DH, H, DH]), ALU.mult).then_inc(kv_ok, 1)

            pool.wait_ge(rows_out, 16 * SEQS)
            pool.wait_ge(idx_ok, 1)

            def gather(s):
                g.indirect_dma_start(rg[:, s % RG, 0:RW], None, rows_dram[:, :],
                                     bass.IndirectOffsetOnAxis(ap=gidx[:, s:s + 1], axis=0)).then_inc(gath[s % RG], 16)

            pool.sem_inc(o_free, RB)
            for s in range(RG):
                gather(s)
            for s in range(SLOTS):
                if s >= 2:
                    pool.wait_ge(scat[(s - 2) % RB], 16 * ((s - 2) // RB) + 16)
                    pool.sem_inc(o_free, 1)
                pool.wait_ge(o_ok, s + 1)
                g.indirect_dma_start(out_rows[:, :], bass.IndirectOffsetOnAxis(ap=sidx[:, s:s + 1], axis=0),
                                     o[:, s % RB, :], None, bounds_check=TOKENS - 1,
                                     oob_is_err=False).then_inc(scat[s % RB], 16)
                if s + RG < AHEAD:
                    gather(s + RG)
            for r in range(RB):
                pool.wait_ge(scat[r], 16 * ((SLOTS - r + RB - 1) // RB))

        @block.scalar
        def _(act):
            a = nc.scalar
            act.dma_start(wcat[:, CQ:CQ + D], wq).then_inc(w_in, 16)
            act.dma_start(wcat[:, CK:CK + D], wk).then_inc(w_in, 16)
            act.dma_start(wcat[:, CV:CV + D], wv).then_inc(w_in, 16)
            act.dma_start(wcat[:, CB:CB + H], wb).then_inc(w_in, 16)
            act.dma_start(small[0:E, :], cent).then_inc(small_in, 16)
            act.dma_start(small[E:2 * E, :], ln_g).then_inc(small_in, 16)
            act.dma_start(small[2 * E:3 * E, :], ln_b).then_inc(small_in, 16)
            act.dma_start(bb_bc[:, :], bb.partition_broadcast(P)).then_inc(small_in, 16)
            act.wait_ge(small_T, 1)
            a.copy(wcat[:, CA:CA + E], small_ps[:, 0:E])
            a.copy(gb[:, :], small_ps[:, E:3 * E]).then_inc(small_ok, 1)

            act.sem_inc(pj_ok, 1)
            with act.Fori(0, SEQS) as b:
                act.wait_ge(va_ok, b + 1)
                a.activation(rs1[:, :], var1[:, :], ACT.Sqrt).then_inc(vr_ok, 1)
                for j in range(TPS + 1):
                    if j < TPS:
                        act.wait_ge(xT_ps_ok, b * TPS + j + 1)
                        a.copy(xT[:, j % 2, :], bank[:, 4 + j % 2, 0:P]).then_inc(xT_ok, 1)
                    if j == 0:
                        act.wait_ge(ss_ok, b + 1)
                    else:
                        n = b * TPS + j - 1
                        act.wait_ge(pj_ps_ok, n + 1)
                        a.copy(proj[:, bass.ds(n, 1), :], bank[:, j - 1:j, 0:PW])
                        last = a.activation(sq[:, j - 1, :], bank[:, j - 1, 0:2 * D], ACT.Square)
                        last.then_inc(pj_ok, 1)
            act.wait_ge(rs2_ok, 1)
            a.activation(rs2[:, :], row[:, :, RRSTD], ACT.Sqrt).then_inc(rs2_ok, 1)
            act.wait_ge(ss_all, 1)
            a.activation(rn_sqrt, rn, ACT.Sqrt).then_inc(ss_sqrt, 1)
            act.wait_ge(logit_ok, 1)
            a.activation(logit[:, :, :], logit[:, :, :], ACT.Sigmoid).then_inc(sig_ok, 1)
            act.wait_ge(mx_ok, 1)
            a.activation(row[:, :, RALPHA], mx[:, :], ACT.Sigmoid).then_inc(alpha_ok, 1)

            def s_and_aT(n, r):
                act.wait_ge(aT_ps_ok, n + 1)
                a.copy(aT[:, r, :], T_ps).then_inc(aT_ok, 1)
                act.wait_ge(s_ps_ok, n + 1)
                a.copy(row[:, n:n + 1, RS:RS + D] if isinstance(n, int) else row[:, bass.ds(n, 1), RS:RS + D],
                       s_ps.unsqueeze(1)).then_inc(s_ok, 1)

            def stage(n, r):
                a.copy(qk[:, r:r + 1, :], proj[:, bass.ds(n, 1), CQ:CQ + 2 * D]).then_inc(qk_ok, 1)

            act.wait_ge(qn_ok, 1)
            act.wait_ge(xrow_ok, SEQS)

            def tiles(b, first):
                for j in range(TPS):
                    stage(b * TPS + j, j % 2)
                    if j:
                        act.wait_ge(qT_ps_ok, b * (TPS - 1) + j)
                        a.copy(qT[:, j % 2, :], T_ps).then_inc(qT_ok, 1)
                    if j or not first:
                        s_and_aT(b * TPS + j - 1, (j - 1) % 2)
            tiles(0, True)
            with act.Fori(1, SEQS) as b:
                tiles(b, False)
            s_and_aT(NT - 1, (NT - 1) % 2)

            act.wait_ge(idx_ok, 1)

            def xlT_of(s, r):
                e = act.value_load(sexp_i[0:1, s:s + 1] if isinstance(s, int) else sexp_i[0:1, bass.ds(s, 1)],
                                   min_val=0, max_val=E - 1)
                act.wait_ge(xlT_ps_ok, s + 1)
                a.activation(xlT[:, r, :], T_ps, ACT.Identity, bias=gb[:, bass.ds(e + E, 1)],
                             scale=gb[:, bass.ds(e, 1)]).then_inc(xlT_ok, 1)
            xlT_of(0, 0)

            def step(s, k):
                if real(s - 3):
                    act.wait_ge(y2_ok, s - 2)
                    a.activation(sg[:, (k - 3) % RB, :], y[:, (k - 3) % RB, :], ACT.Sigmoid).then_inc(sg_ok, 1)
                if real(s):
                    xlT_of(s + 1, (k + 1) % RB)
                if real(s - 1):
                    act.wait_ge(hT_ps_ok, s)
                    a.activation(hT[:, (k - 1) % RB, :, :].rearrange("p c t -> p (c t)"), hT_ps[(k - 1) % RB],
                                 ACT.Relu).then_inc(hT_ok, 1)
            slot_steps(act, step)

        @block.tensor
        def _(pe):
            t = nc.tensor
            pe.wait_ge(const_ok, 1)
            pe.wait_ge(small_in, 64)
            t.transpose(small_ps, small[:, :], ident[0:3 * E, 0:3 * E]).then_inc(small_T, 1)
            pe.wait_ge(small_ok, 1)
            pe.wait_ge(w_in, 64)

            with pe.Fori(0, SEQS) as b:
                pe.wait_ge(xn_ok, b + 1)
                for j in range(TPS + 1):
                    if j < TPS:
                        if j == 0:
                            pe.wait_ge(pj_ok, b * TPS + 1)
                        t.transpose(bank[:, 4 + j % 2, 0:P], xs[:, j, :], ident[:, :]).then_inc(xT_ps_ok, 1)
                    if j:
                        pe.wait_ge(xT_ok, b * TPS + j)
                        t.matmul(bank[:, j - 1, 0:PW], xT[:, (j - 1) % 2, :], wcat[:, :], start=True,
                                 stop=True).then_inc(pj_ps_ok, 1)

            pe.wait_ge(oh_ok, 1)
            oh2 = oh[:, :, :].rearrange("p n e -> p (n e)")
            t.matmul(sum_ps[:, 0:NT * E], before[:, :], oh2, start=True, stop=True)
            t.matmul(sum_ps[:, NT * E:2 * NT * E], ones[:, :], oh2, start=True, stop=True).then_inc(rank_ok, 1)
            pe.wait_ge(oneh_ok, 1)
            for n in range(NT):
                last = t.matmul(inv_ps, ohb[:, n, :], oha[:, n, :, :].rearrange("p a s -> p (a s)"),
                                start=(n == 0), stop=(n == NT - 1))
            last.then_inc(inv_ok, 1)
            pe.wait_ge(idx_ok, 1)
            pe.wait_ge(qn_ok, 1)
            pe.wait_ge(wo_in, 16)
            pe.sem_inc(pre_ok, 2)

            def aT_and_s(b, j):
                n, r = b * TPS + j, j % 2
                pe.wait_ge(red_ok, n + 2)
                if j:
                    pe.wait_ge(attn_ok, b * (TPS - 1) + j)
                t.transpose(T_ps, attn[:, r, :], ident[:, :]).then_inc(aT_ps_ok, 1)
                pe.wait_ge(aT_ok, n + 1)
                if not isinstance(n, int) or n:
                    pe.wait_ge(s_ok, n)
                t.matmul(s_ps, aT[:, r, :], wo_sb[:, :], start=True, stop=True).then_inc(s_ps_ok, 1)

            def tiles(b, first):
                for j in range(TPS):
                    n = b * TPS + j
                    pe.wait_ge(kv_ok, n + 1)
                    pe.wait_ge(m_ok, n + 1)
                    for half in range(2):
                        last = t.matmul(prefix[:, j % 2, half * 512:half * 512 + 512], tri[:, :],
                                        kv[:, j % 2, half * 512:half * 512 + 512], start=True, stop=True)
                    last.then_inc(pre_ok, 1)
                    pe.wait_ge(qk_ok, n + 1)
                    if j:
                        t.transpose(T_ps, qk[:, j % 2, 0:D], ident[:, :]).then_inc(qT_ps_ok, 1)
                    if j == 0:
                        pe.wait_ge(bv_ok, b + 1)
                    if j < TPS - 1:
                        if j == 0 and not first:
                            pe.wait_ge(st_ok, b * (TPS - 1))
                        elif j:
                            pe.wait_ge(st_ok, b * (TPS - 1) + j)
                        t.matmul(st_ps, qk[:, j % 2, D:2 * D],
                                 proj[:, bass.ds(n, 1), CV:CV + D].rearrange("p o c -> p (o c)"), start=(j == 0), stop=True,
                                 skip_group_check=True).then_inc(st_ps_ok, 1)
                    if j:
                        pe.wait_ge(qT_ok, b * (TPS - 1) + j)
                    if j or not first:
                        aT_and_s(*((b, j - 1) if j else (b - 1, TPS - 1)))
                    if j:
                        pe.wait_ge(st_ok, b * (TPS - 1) + j)
                        t.matmul(in_ps, qT[:, j % 2, :], state[:, (j - 1) % 2, :], start=True,
                                 stop=True).then_inc(inter_ok, 1)
            tiles(0, True)
            with pe.Fori(1, SEQS) as b:
                tiles(b, False)
            aT_and_s(SEQS - 1, TPS - 1)

            pe.wait_ge(ffn_in, 64)

            def transpose_x(s, r):
                pe.wait_ge(xl_ok, s + 1)
                t.transpose(T_ps, xl[:, r, :], ident[:, :]).then_inc(xlT_ps_ok, 1)

            def expert(s):
                return pe.value_load(sexp_i[0:1, s:s + 1] if isinstance(s, int) else sexp_i[0:1, bass.ds(s, 1)],
                                     min_val=0, max_val=E - 1)
            transpose_x(0, 0)

            def step(s, k):
                if real(s):
                    e = expert(s)
                    pe.wait_ge(xlT_ok, s + 1)
                    t.matmul(h_ps[k % RB], xlT[:, k % RB, :],
                             w1_sb[:, bass.ds(e, 1), :].rearrange("p o f -> p (o f)"), start=True,
                             stop=True).then_inc(h_ps_ok, 1)
                    transpose_x(s + 1, (k + 1) % RB)
                if real(s - 1):
                    r = (k - 1) % RB
                    pe.wait_ge(h_ok, s)
                    for c in range(FC):
                        last = t.transpose(hT_ps[r][:, c * P:c * P + P], h[:, r, c * P:c * P + P], ident[:, :])
                    last.then_inc(hT_ps_ok, 1)
                if real(s - 2):
                    r = (k - 2) % RB
                    e = expert(s - 2)
                    pe.wait_ge(hT_ok, s - 1)
                    if real(s - 3):
                        pe.wait_ge(y1_ok, s - 2)
                    for c in range(FC):
                        last = t.matmul(y_ps, hT[:, r, c, :],
                                        w2_sb[:, bass.ds(e, 1), c, :].rearrange("p o d -> p (o d)"),
                                        start=(c == 0), stop=(c == FC - 1))
                    last.then_inc(y_ps_ok, 1)
            slot_steps(pe, step)

        @block.vector
        def _(dve):
            v = nc.vector
            chain = [0]

            def link(ins):
                chain[0] += 1
                ins.then_inc(dv, 1)
                dve.wait_ge(dv, chain[0])

            dve.wait_ge(iota_ok, 1)
            link(v.tensor_single_scalar(phead_i[:, :], pidx_i[:, :], 3, ALU.arith_shift_right))
            link(v.tensor_copy(phead[:, :], phead_i[:, :]))
            v.tensor_scalar(same_head[:, :], colhead[:, :, :].rearrange("p h d -> p (h d)"), phead[:, 0:1], None, ALU.is_equal)
            v.tensor_scalar(tri[:, :], col[:, :], pidx[:, 0:1], None, ALU.is_ge)
            v.tensor_scalar(before[:, :], col[:, :], pidx[:, 0:1], None, ALU.is_gt)
            v.memset(ones[:, :], 1.0)
            for z in pe8:
                v.memset(z[:], 0.0)
            v.tensor_scalar(ident[:, :], col[:, :], pidx[:, 0:1], None, ALU.is_equal).then_inc(const_ok, 1)
            dve.sem_inc(ss_ok, 1)

            dve.wait_ge(x_in, 16)

            def joined(st, mean, dif, var):
                return (v.tensor_tensor(mean, st[:, :, 1], st[:, :, 4], ALU.add),
                        v.tensor_tensor(dif, st[:, :, 1], st[:, :, 4], ALU.subtract),
                        v.tensor_tensor(var, st[:, :, 2], st[:, :, 5], ALU.add))

            def halves(mean, dif, var):
                return (v.tensor_scalar(mean, mean, 0.5, None, ALU.mult),
                        v.scalar_tensor_tensor(dif, dif, 0.25, dif, ALU.mult, ALU.mult),
                        v.tensor_scalar(var, var, 1.0 / D, LN_EPS, ALU.mult, ALU.add))

            def layernorm(b):
                def at(j, c, w):
                    return row[:, bass.ds(b * TPS + j, 1), c:c + w].rearrange("p o c -> p (o c)")
                for j in range(TPS):
                    last = v.bn_stats(st1[:, j, :], at(j, RX, D))
                last.then_inc(st1_ok, 1)
                dve.wait_ge(st1_ok, b + 1)
                joined(st1, mean1[:, :], dif1[:, :], var1[:, :])[-1].then_inc(ag1_ok, 1)
                dve.wait_ge(ag1_ok, b + 1)
                halves(mean1[:, :], dif1[:, :], var1[:, :])[-1].then_inc(ag1b_ok, 1)
                dve.wait_ge(ag1b_ok, b + 1)
                v.tensor_tensor(var1[:, :], var1[:, :], dif1[:, :], ALU.add).then_inc(va_ok, 1)
                dve.wait_ge(vr_ok, b + 1)
                v.reciprocal(rs1[:, :], rs1[:, :]).then_inc(va2_ok, 1)
                dve.wait_ge(va2_ok, b + 1)
                v.tensor_tensor(nt1[:, :], var1[:, :], rs1[:, :], ALU.mult).then_inc(na_ok, 1)
                dve.wait_ge(na_ok, b + 1)
                v.scalar_tensor_tensor(nt1[:, :], nt1[:, :], -0.5, rs1[:, :], ALU.mult, ALU.mult).then_inc(nb_ok, 1)
                dve.wait_ge(nb_ok, b + 1)
                v.scalar_tensor_tensor(rs1[:, :], nt1[:, :], 1.5, rs1[:, :], ALU.add, ALU.mult).then_inc(rs1_ok, 1)
                dve.wait_ge(rs1_ok, b + 1)
                if not isinstance(b, int):
                    dve.wait_ge(xrow_ok, b)
                    dve.wait_ge(xT_ps_ok, b * TPS)
                for j in range(TPS):
                    last = v.tensor_scalar(xs[:, j, :], at(j, RX, D), mean1[:, j:j + 1], rs1[:, j:j + 1],
                                           ALU.subtract, ALU.mult)
                last.then_inc(xn_ok, 1)
                dve.wait_ge(xn_ok, b + 1)
                for j in range(TPS):
                    last = v.bn_stats(st2[:, bass.ds(b * TPS + j, 1), :].rearrange("p o c -> p (o c)"), xs[:, j, :])
                last.then_inc(st2_ok, 1)

            def norms(b):
                dve.wait_ge(pj_ok, b * TPS + TPS + 1)
                rn = rnorm[:, bass.ds(b * TPS, TPS), :]
                v.tensor_reduce(rn, sq[:, :, :].rearrange("p j (h d) -> p j h d", d=DH), AX.X, ALU.add).then_inc(ss_ok, 1)

            layernorm(0)
            with dve.Fori(0, SEQS - 1) as b:
                layernorm(b + 1)
                norms(b)
            norms(SEQS - 1)
            v.tensor_tensor(logit[:, :, :], proj[:, :, CB:CB + H], bb_bc[:, :].unsqueeze(1).to_broadcast([P, NT, H]),
                            ALU.add).then_inc(logit_ok, 1)
            dve.wait_ge(ss_ok, SEQS + 1)
            v.tensor_scalar(rnorm[:, :, :], rnorm[:, :, :], NORM_EPS2, None, ALU.max).then_inc(ss_all, 1)
            dve.wait_ge(st2_ok, SEQS)
            link(joined(st2, row[:, :, RMEAN], nt2[:, :], row[:, :, RRSTD])[-1])
            link(halves(row[:, :, RMEAN], nt2[:, :], row[:, :, RRSTD])[-1])
            v.tensor_tensor(row[:, :, RRSTD], row[:, :, RRSTD], nt2[:, :], ALU.add).then_inc(rs2_ok, 1)
            aff = proj[:, :, CA:CA + E]

            def over_tiles(ap):
                return ap.unsqueeze(1).to_broadcast([P, NT, E])

            def over_experts(ap):
                return ap.unsqueeze(2).to_broadcast([P, NT, E])

            v.tensor_reduce(mx[:, :], aff, AX.X, ALU.max).then_inc(mx_ok, 1)
            dve.wait_ge(mx_ok, 1)
            link(v.tensor_tensor(eq[:, :, :], aff, over_experts(mx[:, :]), ALU.is_equal))
            dve.wait_ge(rs2_ok, 2)
            dve.wait_ge(ss_sqrt, 1)
            v.reciprocal(rs2[:, :], rs2[:, :])
            link(v.reciprocal(rn_sqrt, rn_sqrt))
            v.tensor_tensor(nt2[:, :], row[:, :, RRSTD], rs2[:, :], ALU.mult)
            link(v.tensor_tensor(rn, rn, rn_sqrt, ALU.mult))
            v.scalar_tensor_tensor(nt2[:, :], nt2[:, :], -0.5, rs2[:, :], ALU.mult, ALU.mult)
            link(v.scalar_tensor_tensor(rn, rn, -0.5, rn_sqrt, ALU.mult, ALU.mult))
            v.scalar_tensor_tensor(row[:, :, RRSTD], nt2[:, :], 1.5, rs2[:, :], ALU.add, ALU.mult).then_inc(rs2_all, 1)
            link(v.scalar_tensor_tensor(rn, rn, 1.5, rn_sqrt, ALU.add, ALU.mult))
            dve.wait_ge(sig_ok, 1)
            v.tensor_tensor(rnorm[:, :, H:2 * H], rnorm[:, :, H:2 * H], logit[:, :, :], ALU.mult).then_inc(bvs_ok, 1)
            q4 = proj[:, :, CQ:CQ + D].rearrange("p n (h d) -> p n h d", d=DH)
            v.tensor_tensor(q4, q4, rnorm[:, :, 0:H].unsqueeze(3).to_broadcast([P, NT, H, DH]), ALU.mult).then_inc(qn_ok, 1)
            link(v.tensor_tensor(eq[:, :, :], eq[:, :, :], over_tiles(rev[:, :]), ALU.mult))
            link(v.tensor_reduce(mw[:, :], eq[:, :, :], AX.X, ALU.max))
            v.tensor_tensor(oh[:, :, :], eq[:, :, :], over_experts(mw[:, :]), ALU.is_equal).then_inc(oh_ok, 1)
            for z in pre:
                v.memset(z[:, 0:PAD, :], 0.0)
            dve.wait_ge(rank_ok, 1)
            link(v.tensor_copy(pre[0][:, PAD:, :].rearrange("p n e -> p (n e)"), sum_ps[:, NT * E:2 * NT * E]))
            src = 0
            for shift in (1, 2, 4, 8, 16):
                link(v.tensor_tensor(pre[1 - src][:, PAD:, :], pre[src][:, PAD:, :], pre[src][:, PAD - shift:PAD + NT - shift, :],
                                     ALU.add))
                src = 1 - src
            link(v.tensor_tensor(cmp[:, :, :], pre[src][:, PAD + NT - 1, :].unsqueeze(2).to_broadcast([P, E, NT]),
                                 steps[:, :].unsqueeze(1).to_broadcast([P, E, NT]), ALU.is_gt))
            link(v.tensor_reduce(pe8[0][:, 4:], cmp[:, :, :], AX.X, ALU.add))
            es = 0
            for shift in (1, 2, 4):
                link(v.tensor_tensor(pe8[1 - es][:, 4:], pe8[es][:, 4:], pe8[es][:, 4 - shift:4 + E - shift], ALU.add))
                es = 1 - es
            link(v.scalar_tensor_tensor(eq[:, :, :], over_tiles(pe8[es][:, 3:3 + E]), float(P),
                                        pre[src][:, PAD - 1:PAD + NT - 1, :], ALU.mult, ALU.add))
            link(v.tensor_tensor(eq[:, :, :].rearrange("p n e -> p (n e)"), eq[:, :, :].rearrange("p n e -> p (n e)"),
                                 sum_ps[:, 0:NT * E], ALU.add))
            link(v.tensor_tensor(eq[:, :, :], eq[:, :, :], oh[:, :, :], ALU.mult))
            link(v.tensor_reduce(pos[:, :], eq[:, :, :], AX.X, ALU.add))
            link(v.tensor_copy(pos_i[:, :], pos[:, :]))
            v.tensor_single_scalar(pa_i[:, :], pos_i[:, :], 7, ALU.arith_shift_right)
            link(v.tensor_single_scalar(pb_i[:, :], pos_i[:, :], P - 1, ALU.bitwise_and))
            v.tensor_copy(pa[:, :], pa_i[:, :])
            link(v.tensor_copy(pb[:, :], pb_i[:, :]))
            valid = oha[:, :, 2, :]
            v.tensor_tensor(valid, slotno[:, :].unsqueeze(1).to_broadcast([P, NT, AHEAD]),
                            pa[:, :].unsqueeze(2).to_broadcast([P, NT, AHEAD]), ALU.is_equal)
            link(v.tensor_tensor(ohb[:, :, :], col[:, :].unsqueeze(1).to_broadcast([P, NT, P]),
                                 pb[:, :].unsqueeze(2).to_broadcast([P, NT, P]), ALU.is_equal))
            v.tensor_scalar(oha[:, :, 0, :], valid, pidx[:, 0:1], None, ALU.mult)
            v.tensor_tensor(oha[:, :, 1, :], valid, tileno[:, :].unsqueeze(2).to_broadcast([P, NT, AHEAD]),
                            ALU.mult).then_inc(oneh_ok, 1)
            link(v.tensor_tensor(scmp[:, :, :], slotno[0:1, :].unsqueeze(2).to_broadcast([1, AHEAD, E - 1]),
                                 pe8[es][0:1, 4:4 + E - 1].unsqueeze(1).to_broadcast([1, AHEAD, E - 1]), ALU.is_ge))
            link(v.tensor_reduce(sexp[:, :], scmp[:, :, :], AX.X, ALU.add))
            v.tensor_copy(sexp_i[:, :], sexp[:, :])
            dve.wait_ge(inv_ok, 1)
            link(v.tensor_copy(inv[:, :, :].rearrange("p a s -> p (a s)"), inv_ps))
            v.scalar_tensor_tensor(tok[:, :], inv[:, 1, :], float(P), inv[:, 0, :], ALU.mult, ALU.add)
            link(v.tensor_scalar(past[:, :], inv[:, 2, :], -NOWHERE, NOWHERE, ALU.mult, ALU.add))
            link(v.tensor_tensor(past[:, :], past[:, :], tok[:, :], ALU.add))
            v.tensor_copy(gidx[:, :], tok[:, :])
            v.tensor_copy(sidx[:, :], past[:, :]).then_inc(idx_ok, 1)

            dve.sem_inc(m_ok, 2)
            dve.sem_inc(red_ok, 1)

            def tiles(b):
                for j in range(TPS):
                    n = b * TPS + j
                    q3 = proj[:, bass.ds(n, 1), CQ:CQ + D].rearrange("p o (h d) -> p (o d) h", d=DH)
                    dve.wait_ge(red_ok, n + 1)
                    dve.wait_ge(pre_ok, n + 3)
                    v.tensor_tensor(m[:, :].rearrange("p (d h e) -> p d h e", d=DH, h=H),
                                    prefix[:, j % 2, :].rearrange("p (d h e) -> p d h e", d=DH, h=H),
                                    q3.unsqueeze(3).to_broadcast([P, DH, H, DH]), ALU.mult).then_inc(m_ok, 1)
                    if j < TPS - 1:
                        dve.wait_ge(st_ps_ok, b * (TPS - 1) + j + 1)
                        v.tensor_tensor(state[:, j % 2, :], st_ps, same_head[:, :], ALU.mult).then_inc(st_ok, 1)
                    dve.wait_ge(m_ok, n + 3)
                    red = v.tensor_reduce(attn[:, j % 2, :], m[:, :].rearrange("p (d c) -> p c d", d=DH), AX.X, ALU.add)
                    red.then_inc(red_ok, 1)
                    if j:
                        dve.wait_ge(inter_ok, b * (TPS - 1) + j)
                        dve.wait_ge(red_ok, n + 2)
                        v.tensor_tensor(attn[:, j % 2, :], attn[:, j % 2, :], in_ps, ALU.add).then_inc(attn_ok, 1)
            with dve.Fori(0, SEQS) as b:
                tiles(b)

            dve.wait_ge(ffn_in, 64)

            def expert(s):
                return dve.value_load(sexp_i[0:1, s:s + 1] if isinstance(s, int) else sexp_i[0:1, bass.ds(s, 1)],
                                      min_val=0, max_val=E - 1)

            def second_norm(s, k):
                dve.wait_ge(gath[k % RG], 16 * rounds(s, k, RG) + 16)
                v.tensor_scalar(xl[:, k % RB, :], rg[:, k % RG, RN:RN + D], rg[:, k % RG, RMEAN:RMEAN + 1],
                                rg[:, k % RG, RRSTD:RRSTD + 1], ALU.subtract, ALU.mult).then_inc(xl_ok, 1)

            def rounds(s, k, n):
                if isinstance(s, int):
                    return s // n
                return its[0] * (RG // n) + k // n
            its = [0]
            second_norm(0, 0)

            def step(s, k):
                if real(s):
                    second_norm(s + 1, k + 1)
                    e = expert(s)
                    dve.wait_ge(h_ps_ok, s + 1)
                    v.tensor_tensor(h[:, k % RB, :], h_ps[k % RB], b1_bc[:, bass.ds(e, 1), :].rearrange("p o f -> p (o f)"),
                                    ALU.add).then_inc(h_ok, 1)
                a, ra, ga = real(s - 3), (k - 3) % RB, (k - 3) % RG
                c, rc, gc = real(s - 2), (k - 2) % RB, (k - 2) % RG
                if a:
                    dve.wait_ge(sg_ok, s - 2)
                    v.tensor_tensor(y[:, ra, :], y[:, ra, :], sg[:, ra, :], ALU.mult).then_inc(y3_ok, 1)
                if c:
                    e = expert(s - 2)
                    dve.wait_ge(y_ps_ok, s - 1)
                    v.tensor_tensor(y[:, rc, :], y_ps, b2_bc[:, bass.ds(e, 1), :].rearrange("p o d -> p (o d)"),
                                    ALU.add).then_inc(y1_ok, 1)
                if a:
                    dve.wait_ge(y3_ok, s - 2)
                    v.tensor_tensor(y[:, ra, :], y[:, ra, :], rg[:, ga, RS:RS + D], ALU.mult).then_inc(y4_ok, 1)
                if c:
                    dve.wait_ge(y1_ok, s - 1)
                    v.scalar_tensor_tensor(y[:, rc, :], y[:, rc, :], rg[:, gc, RALPHA:RALPHA + 1], rg[:, gc, RN:RN + D],
                                           ALU.mult, ALU.add).then_inc(y2_ok, 1)
                if a:
                    dve.wait_ge(y4_ok, s - 2)
                    dve.wait_ge(o_free, s - 2)
                    v.tensor_tensor(o[:, ra, :], y[:, ra, :], rg[:, ga, RX:RX + D], ALU.add).then_inc(o_ok, 1)

            for s in range(FIRST):
                step(s, s)
            with dve.Fori(0, (SLOTS - FIRST) // RG) as it:
                its[0] = it
                for k in range(FIRST, FIRST + RG):
                    step(it * RG + k, k)
            for s in range(SLOTS, SLOTS + FIRST):
                step(s, s)


_INS = ["L0_attn_x", "L0_attn_Wq", "L0_attn_Wk", "L0_attn_Wv", "L0_attn_Wo", "L0_attn_Wb", "L0_attn_bb",
        "L0_ffn_centroids", "L0_ffn_ln_g", "L0_ffn_ln_b", "L0_ffn_w1", "L0_ffn_b1", "L0_ffn_w2", "L0_ffn_b2"]


def kernel(**inputs):
    import numpy as _np
    import concourse.bacc as _bacc
    from concourse.bass_utils import run_bass_kernel_spmd as _run

    nc = _bacc.Bacc("TRN2", target_bir_lowering=False, num_devices=1)
    arrays, args = {}, []
    for name in _INS:
        a = _np.ascontiguousarray(inputs[name])
        arrays[f"in_{name}"] = a
        args.append(nc.dram_tensor(f"in_{name}", a.shape, mybir.dt.from_np(a.dtype), kind="ExternalInput").ap())
    args.append(nc.dram_tensor("out_dram", (SEQS, SEQ, D), F32, kind="ExternalOutput").ap())
    build(nc, *args)
    r = _run(nc, [arrays], core_ids=[0])
    return r.results[0]["out_dram"]
```

```python
from contextlib import ExitStack

import concourse.bass as bass
from concourse import mybir

F32 = mybir.dt.float32
BF16 = mybir.dt.bfloat16
I32 = mybir.dt.int32
ALU = mybir.AluOpType
ACT = mybir.ActivationFunctionType
AX = mybir.AxisListType

P = 128
D = 128
H, DH = 16, 8
SEQS, SEQ = 8, 512
NT = SEQS * SEQ // P
TPS = SEQ // P
E, F = 8, 512
FC = F // P
TOKENS = NT * P
SLOTS = NT + E - 1
LEAD = 2
ALL = SLOTS + LEAD
KVW = DH * H * DH
BANK = 512
CQ, CK, CV, CB, CA = 0, D, 2 * D, 3 * D, 3 * D + H
PW = CA + E
RX, RS, RALPHA, RSC1, RSH1, RSC2, RSH2 = 0, D, 2 * D, 2 * D + 1, 2 * D + 2, 2 * D + 3, 2 * D + 4
RW = 2 * D + 5
LN_EPS = 1e-5
NORM_EPS2 = 1e-24
NOWHERE = 8192.0
RB = 3
RG = 9
FIRST = 3


def build(nc, x, wq, wk, wv, wo, wb, bb, cent, ln_g, ln_b, w1, b1, w2, b2, out):
    rows_dram = nc.dram_tensor("token_rows", (TOKENS, RW), F32).ap()
    xt = x.rearrange("s (j p) d -> p (s j) d", p=P)
    out_rows = out.rearrange("s l d -> (s l) d")
    ctx = ExitStack()
    with ctx:
        def sb(name, shape, dt=F32):
            return ctx.enter_context(nc.sbuf_tensor(name, shape, dt))

        def sem(name):
            return ctx.enter_context(nc.semaphore(name))

        row = sb("row", [P, NT, RW])
        proj = sb("proj", [P, NT, PW])
        wcat = sb("wcat", [D, PW])
        wo_sb = sb("wo_sb", [D, D])
        small = sb("small", [3 * E, D])
        gb = sb("gb", [D, 2 * E])
        bb_bc = sb("bb_bc", [P, H])
        w1_sb = sb("w1_sb", [D, E, F])
        w2_sb = sb("w2_sb", [P, E, FC, D])
        b1_bc = sb("b1_bc", [P, E, F])
        b2_bc = sb("b2_bc", [P, E, D])
        col = sb("col", [P, D])
        colhead = sb("colhead", [P, H, DH])
        pidx = sb("pidx", [P, 1])
        pidx_i = sb("pidx_i", [P, 1], I32)
        phead_i = sb("phead_i", [P, 1], I32)
        phead = sb("phead", [P, 1])
        rev = sb("rev", [P, E])
        steps = sb("steps", [P, NT])
        tileno = sb("tileno", [P, NT])
        slotno = sb("slotno", [P, ALL])
        ident = sb("ident", [P, P])
        tri = sb("tri", [P, P])
        before = sb("before", [P, P], BF16)
        ones = sb("ones", [P, P], BF16)
        same_head = sb("same_head", [P, P])
        st1 = sb("st1", [P, NT, 6])
        st2 = sb("st2", [P, NT, 6])
        mean1 = sb("mean1", [P, NT])
        var1 = sb("var1", [P, NT])
        mean2 = sb("mean2", [P, NT])
        var2 = sb("var2", [P, NT])
        tmp = sb("tmp", [P, NT])
        xs = sb("xs", [P, TPS, D])
        qk = xs[:, :, :].rearrange("p (i a) c -> p i (a c)", i=2)
        xT = sb("xT", [D, 2, P])
        m = sb("m", [P, KVW])
        sq = m[:, :].rearrange("p (j c) -> p j c", j=TPS)
        ss = sb("ss", [P, NT, 2, H])
        rnorm = sb("rnorm", [P, NT, 2, H])
        mx = sb("mx", [P, NT])
        mw = sb("mw", [P, NT])
        oh = sb("oh", [P, NT, E], BF16)
        pe8 = [sb(f"pe8{i}", [P, 4 + E]) for i in range(2)]
        pos = sb("pos", [P, NT])
        pos_i = sb("pos_i", [P, NT], I32)
        pa_i = sb("pa_i", [P, NT], I32)
        pb_i = sb("pb_i", [P, NT], I32)
        pa = sb("pa", [P, NT])
        pb = sb("pb", [P, NT])
        inv = sb("inv", [P, 3, ALL])
        tok = sb("tok", [P, ALL])
        past = sb("past", [P, ALL])
        gidx = sb("gidx", [P, ALL], I32)
        sidx = sb("sidx", [P, ALL], I32)
        scmp = sb("scmp", [1, ALL, E - 1])
        sexp = sb("sexp", [1, ALL])
        sexp_i = sb("sexp_i", [1, ALL], I32)
        WORK = RB * (2 * F + 5 * D) + RG * D
        work = sb("work", [P, WORK])
        used = [0]

        def part(words):
            used[0] += words
            assert used[0] <= WORK
            return work[:, used[0] - words:used[0]]

        logit = part(NT * H).rearrange("p (n h) -> p n h", n=NT)
        tmp_n = part(NT * 2 * H).rearrange("p (n a h) -> p n a h", n=NT, a=2)
        eq = part(NT * E).rearrange("p (n e) -> p n e", n=NT)
        cmp = part(NT * E).rearrange("p (e n) -> p e n", e=E)
        ohb = part(NT * P // 2).bitcast(BF16).rearrange("p (n c) -> p n c", n=NT)
        oha = part(NT * 3 * ALL // 2).bitcast(BF16).rearrange("p (n a s) -> p n a s", n=NT, a=3)
        kv = sb("kv", [P, 2, KVW])
        attn = sb("attn", [P, 2, D])
        state = sb("state", [P, TPS - 1, D])
        qT = sb("qT", [P, 2, P])
        aT = xT
        rg = proj
        used[0] = 0
        xl, xlT, y, sg, o = (part(RB * D).rearrange("p (r c) -> p r c", r=RB) for _ in range(5))
        h = part(RB * F).rearrange("p (r f) -> p r f", r=RB)
        hT = part(RB * F).rearrange("p (r c t) -> p r c t", r=RB, c=FC)
        xn = part(RG * D).rearrange("p (r c) -> p r c", r=RG)
        u = kv[:, 0, 0:RB * D].rearrange("p (r c) -> p r c", r=RB)

        bank = ctx.enter_context(nc.psum_tensor("bank", [P, 8, BANK], F32))
        prefix = bank[:, 0:4, :].rearrange("p (i a) c -> p i (a c)", i=2)
        small_ps = bank[:, 6, 0:3 * E]
        rank_ps = bank[:, 6, 0:NT * E]
        total_ps = bank[:, 7, 0:E]
        inv_ps = bank[:, 7, 0:3 * ALL]
        st_ps = bank[:, 4, 0:D]
        qT_ps = bank[:, 5, 0:P]
        aT_ps = bank[:, 6, 0:P]
        s_ps = bank[:, 7, 0:D]
        h_ps = [bank[:, i, :] for i in (0, 1, 2)]
        hT_ps = [bank[:, i, :] for i in (3, 4, 6)]
        xlT_ps = bank[:, 5, 0:P]
        y_ps = bank[:, 7, 0:D]

        names = """w_in small_in wo_in ffn_in iota_ok const_ok small_T small_ok dv
            st1_ok var1_ok sqrt1_ok scale1_ok xs_ok st2_ok xT_ps_ok xT_ok pj_ps_ok pj_ok sq_ok
            sum_ok ss_ok ln2_ok logit_ok lnk_ok lnq_ok r2_ok sig_ok mx_ok alpha_ok pl bvs_ok q_scale_ok scalars_ok
            oh_ok rank_ok oneh_ok inv_ok idx_ok
            bv_ok qn_ok kv_ok pre_ok m_ok red_ok qk_ok qT_ps_ok qT_ok st_ps_ok st_ok aT_ps_ok aT_ok s_ps_ok s_ok rows_out
            xn_ok xl_ok xlT_ps_ok xlT_ok h_ps_ok h_ok hT_ps_ok hT_ok y_ps_ok y1_ok z_ok u_ok sg_ok y2_ok o_ok o_free"""
        S = {n: sem(n) for n in names.split()}
        (w_in, small_in, wo_in, ffn_in, iota_ok, const_ok, small_T, small_ok, dv,
         st1_ok, var1_ok, sqrt1_ok, scale1_ok, xs_ok, st2_ok, xT_ps_ok, xT_ok, pj_ps_ok, pj_ok, sq_ok,
         sum_ok, ss_ok, ln2_ok, logit_ok, lnk_ok, lnq_ok, r2_ok, sig_ok, mx_ok, alpha_ok, pl, bvs_ok, q_scale_ok, scalars_ok,
         oh_ok, rank_ok, oneh_ok, inv_ok, idx_ok,
         bv_ok, qn_ok, kv_ok, pre_ok, m_ok, red_ok, qk_ok, qT_ps_ok, qT_ok, st_ps_ok, st_ok, aT_ps_ok, aT_ok, s_ps_ok,
         s_ok, rows_out,
         xn_ok, xl_ok, xlT_ps_ok, xlT_ok, h_ps_ok, h_ok, hT_ps_ok, hT_ok, y_ps_ok, y1_ok, z_ok, u_ok, sg_ok, y2_ok,
         o_ok, o_free) = S.values()
        x_in = [sem(f"x_in{i}") for i in range(SEQS)]
        gath = [sem(f"gath{i}") for i in range(RG)]
        scat = [sem(f"scat{i}") for i in range(RB)]

        def real(s):
            return not isinstance(s, int) or 0 <= s < SLOTS

        def slot_steps(eng, step):
            def reader(known):
                def expert_of(s, k):
                    if k not in known:
                        at = sexp_i[0:1, s:s + 1] if isinstance(s, int) else sexp_i[0:1, bass.ds(s, 1)]
                        known[k] = eng.value_load(at, min_val=0, max_val=E - 1)
                    return known[k]
                return expert_of
            expert_of = reader({})
            for s in range(FIRST):
                step(s, s, 0, expert_of)
            with eng.Fori(0, (SLOTS - FIRST) // RG) as it:
                expert_of = reader({})
                for k in range(FIRST, FIRST + RG):
                    step(it * RG + k, k, it, expert_of)
            expert_of = reader({})
            for s in range(SLOTS, SLOTS + FIRST):
                step(s, s, 0, expert_of)

        block = ctx.enter_context(nc.Block())

        @block.sync
        def _(sp):
            for b in range(SEQS):
                sp.dma_start(row[:, b * TPS:(b + 1) * TPS, RX:RX + D], xt[:, b * TPS:(b + 1) * TPS, :]).then_inc(x_in[b], 16)
            sp.dma_start(wo_sb[:, :], wo).then_inc(wo_in, 16)
            sp.dma_start(w1_sb[:, :, :], w1.rearrange("e d f -> d e f")).then_inc(ffn_in, 16)
            sp.dma_start(w2_sb[:, :, :, :], w2.rearrange("e (c p) d -> p e c d", p=P)).then_inc(ffn_in, 16)
            sp.dma_start(b1_bc[:, :, :], b1.partition_broadcast(P)).then_inc(ffn_in, 16)
            sp.dma_start(b2_bc[:, :, :], b2.partition_broadcast(P)).then_inc(ffn_in, 16)
            sp.wait_ge(alpha_ok, 1)
            sp.wait_ge(scalars_ok, 1)
            with sp.Fori(0, SEQS) as b:
                sp.wait_ge(s_ok, b * TPS + TPS)
                sp.dma_start(rows_dram[bass.ds(b * SEQ, SEQ), :].rearrange("(j p) c -> p j c", p=P),
                             row[:, bass.ds(b * TPS, TPS), :]).then_inc(rows_out, 16)

        @block.gpsimd
        def _(pool):
            g = nc.gpsimd

            def iota(ap, pattern, base=0, per_partition=0):
                return g.iota(ap, pattern, base=base, channel_multiplier=per_partition, allow_small_or_imprecise_dtypes=True)
            iota(pidx_i[:, :], [[0, 1]], per_partition=1)
            iota(col[:, :], [[1, D]])
            iota(pidx[:, :], [[0, 1]], per_partition=1)
            iota(colhead[:, :, :], [[1, H], [0, DH]])
            iota(rev[:, :], [[-1, E]], base=E)
            iota(steps[:, :], [[P, NT]])
            iota(tileno[:, :], [[1, NT]])
            iota(slotno[:, :], [[1, ALL]]).then_inc(iota_ok, 1)
            pool.sem_inc(sq_ok, 1)
            with pool.Fori(0, SEQS) as b:
                pool.wait_ge(pj_ok, b * TPS + TPS + 1)
                pool.wait_ge(sum_ok, b + 1)
                p4 = proj[:, bass.ds(b * TPS, TPS), CQ:CQ + 2 * D]
                g.tensor_tensor(sq, p4, p4, ALU.mult).then_inc(sq_ok, 1)
            pool.wait_ge(lnq_ok, 1)
            a_q, r_q, t_q = ss[:, :, 0, :], rnorm[:, :, 0, :], tmp_n[:, :, 0, :]
            g.tensor_tensor(t_q, r_q, r_q, ALU.mult).then_inc(pl, 1)
            pool.wait_ge(pl, 1)
            g.tensor_tensor(t_q, t_q, a_q, ALU.mult).then_inc(pl, 1)
            pool.wait_ge(pl, 2)
            g.tensor_scalar(t_q, t_q, -0.5, 1.5, ALU.mult, ALU.add).then_inc(pl, 1)
            pool.wait_ge(pl, 3)
            g.tensor_tensor(r_q, r_q, t_q, ALU.mult).then_inc(q_scale_ok, 1)
            pool.wait_ge(q_scale_ok, 1)

            def scale_values(b):
                v4 = proj[:, bass.ds(b * TPS, TPS), CV:CV + D].rearrange("p j (h e) -> p j h e", e=DH)
                g.tensor_tensor(v4, v4, rnorm[:, bass.ds(b * TPS, TPS), 1, :].unsqueeze(3).to_broadcast([P, TPS, H, DH]),
                                ALU.mult).then_inc(bv_ok, 1)

            def norm_queries(b):
                q4 = proj[:, bass.ds(b * TPS, TPS), CQ:CQ + D].rearrange("p j (h d) -> p j h d", d=DH)
                g.tensor_tensor(q4, q4, rnorm[:, bass.ds(b * TPS, TPS), 0, :].unsqueeze(3).to_broadcast([P, TPS, H, DH]),
                                ALU.mult).then_inc(qn_ok, 1)

            def outer_products(b, ahead):
                pool.wait_ge(bv_ok, b + 1)
                for j in range(TPS):
                    n = b * TPS + j
                    pool.wait_ge(pre_ok, n + 1)
                    k3 = proj[:, bass.ds(n, 1), CK:CK + D].rearrange("p o (h d) -> p (o d) h", d=DH)
                    v3 = proj[:, bass.ds(n, 1), CV:CV + D].rearrange("p o (h e) -> p (o h) e", e=DH)
                    g.tensor_tensor(kv[:, j % 2, :].rearrange("p (d h e) -> p d h e", d=DH, h=H),
                                    k3.unsqueeze(3).to_broadcast([P, DH, H, DH]),
                                    v3.unsqueeze(1).to_broadcast([P, DH, H, DH]), ALU.mult).then_inc(kv_ok, 1)
                    if ahead and j == 1:
                        scale_values(b + 1)
                    if ahead and j == 2:
                        norm_queries(b + 1)

            pool.wait_ge(bvs_ok, 1)
            scale_values(0)
            norm_queries(0)
            with pool.Fori(0, SEQS - 1) as b:
                outer_products(b, True)
            outer_products(SEQS - 1, False)

            pool.wait_ge(rows_out, 16 * SEQS)
            pool.wait_ge(idx_ok, 1)
            pool.sem_inc(o_free, RB)

            def gather(s):
                g.indirect_dma_start(rg[:, s % RG, 0:RW], None, rows_dram[:, :],
                                     bass.IndirectOffsetOnAxis(ap=gidx[:, s:s + 1], axis=0)).then_inc(gath[s % RG], 16)

            for s in range(RG):
                gather(s)
            for s in range(SLOTS):
                if s >= 2:
                    pool.wait_ge(scat[(s - 2) % RB], 16 * ((s - 2) // RB) + 16)
                    pool.sem_inc(o_free, 1)
                pool.wait_ge(o_ok, s + 1)
                g.indirect_dma_start(out_rows[:, :], bass.IndirectOffsetOnAxis(ap=sidx[:, s:s + 1], axis=0),
                                     o[:, s % RB, :], None, bounds_check=TOKENS - 1,
                                     oob_is_err=False).then_inc(scat[s % RB], 16)
                if s + RG < ALL:
                    gather(s + RG)
            for r in range(RB):
                pool.wait_ge(scat[r], 16 * ((SLOTS - r + RB - 1) // RB))

        @block.scalar
        def _(act):
            a = nc.scalar
            act.dma_start(wcat[:, CQ:CQ + D], wq).then_inc(w_in, 16)
            act.dma_start(wcat[:, CK:CK + D], wk).then_inc(w_in, 16)
            act.dma_start(wcat[:, CV:CV + D], wv).then_inc(w_in, 16)
            act.dma_start(wcat[:, CB:CB + H], wb).then_inc(w_in, 16)
            act.dma_start(small[0:E, :], cent).then_inc(small_in, 16)
            act.dma_start(small[E:2 * E, :], ln_g).then_inc(small_in, 16)
            act.dma_start(small[2 * E:3 * E, :], ln_b).then_inc(small_in, 16)
            act.dma_start(bb_bc[:, :], bb.partition_broadcast(P)).then_inc(small_in, 16)
            act.wait_ge(small_T, 1)
            a.copy(wcat[:, CA:CA + E], small_ps[:, 0:E])
            a.copy(gb[:, :], small_ps[:, E:3 * E]).then_inc(small_ok, 1)
            act.wait_ge(var1_ok, 1)
            a.activation(tmp[:, :], var1[:, :], ACT.Ln).then_inc(sqrt1_ok, 1)
            act.wait_ge(sqrt1_ok, 1)
            a.activation(row[:, :, RSC1], tmp[:, :], ACT.Exp, scale=-0.5).then_inc(sqrt1_ok, 1)

            act.sem_inc(pj_ok, 1)
            with act.Fori(0, SEQS) as b:
                for j in range(TPS + 1):
                    if j < TPS:
                        act.wait_ge(xT_ps_ok, b * TPS + j + 1)
                        a.copy(xT[:, j % 2, :], bank[:, 4 + j % 2, 0:P]).then_inc(xT_ok, 1)
                    if j:
                        n = b * TPS + j - 1
                        act.wait_ge(pj_ps_ok, n + 1)
                        a.copy(proj[:, bass.ds(n, 1), :], bank[:, j - 1:j, 0:PW]).then_inc(pj_ok, 1)
            act.wait_ge(ss_ok, SEQS)
            a.activation(tmp_n[:, :, 1, :], ss[:, :, 1, :], ACT.Ln).then_inc(lnk_ok, 1)
            a.activation(tmp_n[:, :, 0, :], ss[:, :, 0, :], ACT.Ln).then_inc(lnk_ok, 1)
            act.wait_ge(ln2_ok, 1)
            a.activation(tmp[:, :], var2[:, :], ACT.Ln).then_inc(r2_ok, 1)
            act.wait_ge(lnk_ok, 2)
            a.activation(rnorm[:, :, 1, :], tmp_n[:, :, 1, :], ACT.Exp, scale=-0.5).then_inc(lnk_ok, 1)
            a.activation(rnorm[:, :, 0, :], tmp_n[:, :, 0, :], ACT.Exp, scale=-0.5).then_inc(lnq_ok, 1)
            act.wait_ge(r2_ok, 1)
            a.activation(row[:, :, RSC2], tmp[:, :], ACT.Exp, scale=-0.5).then_inc(r2_ok, 1)
            act.wait_ge(logit_ok, 1)
            a.activation(logit, logit, ACT.Sigmoid).then_inc(sig_ok, 1)
            act.wait_ge(mx_ok, 1)
            a.activation(row[:, :, RALPHA], mx[:, :], ACT.Sigmoid).then_inc(alpha_ok, 1)

            act.wait_ge(xT_ps_ok, NT)

            def out_s(n, r):
                act.wait_ge(s_ps_ok, n + 1)
                a.copy(row[:, bass.ds(n, 1), RS:RS + D], s_ps.unsqueeze(1)).then_inc(s_ok, 1)

            def out_aT(n, r):
                act.wait_ge(aT_ps_ok, n + 1)
                a.copy(aT[:, r, :], aT_ps).then_inc(aT_ok, 1)

            def tiles(b, first):
                act.wait_ge(qn_ok, b + 1)
                for j in range(TPS):
                    n = b * TPS + j
                    a.copy(qk[:, j % 2:j % 2 + 1, :], proj[:, bass.ds(n, 1), CQ:CQ + 2 * D]).then_inc(qk_ok, 1)
                    if j:
                        act.wait_ge(qT_ps_ok, b * (TPS - 1) + j)
                        a.copy(qT[:, j % 2, :], qT_ps).then_inc(qT_ok, 1)
                    if j >= 1 or not first:
                        out_aT(n - 1, (j - 1) % 2)
                    if j >= 2 or not first:
                        out_s(n - 2, j % 2)
            tiles(0, True)
            with act.Fori(1, SEQS) as b:
                tiles(b, False)
            out_aT(NT - 1, (NT - 1) % 2)
            out_s(NT - 2, 0)
            out_s(NT - 1, 1)

            act.wait_ge(idx_ok, 1)

            def layernorm_1(s, k, rounds):
                act.wait_ge(gath[k % RG], (rounds + k // RG) * 16 + 16)
                r = rg[:, k % RG, :]
                a.activation(xn[:, k % RG, :], r[:, RX:RX + D], ACT.Identity, bias=r[:, RSH1:RSH1 + 1],
                             scale=r[:, RSC1:RSC1 + 1]).then_inc(xn_ok, 1)

            def layernorm_2(s, k):
                act.wait_ge(xn_ok, s + 1)
                r = rg[:, k % RG, :]
                a.activation(xl[:, k % RB, :], xn[:, k % RG, :], ACT.Identity, bias=r[:, RSH2:RSH2 + 1],
                             scale=r[:, RSC2:RSC2 + 1]).then_inc(xl_ok, 1)

            def gain_and_shift(s, k, expert_of):
                e = expert_of(s, k)
                act.wait_ge(xlT_ps_ok, s + 1)
                a.activation(xlT[:, k % RB, :], xlT_ps, ACT.Identity, bias=gb[:, bass.ds(e + E, 1)],
                             scale=gb[:, bass.ds(e, 1)]).then_inc(xlT_ok, 1)

            for s in range(LEAD):
                layernorm_1(s, s, 0)
                layernorm_2(s, s)
            e0 = act.value_load(sexp_i[0:1, 0:1], min_val=0, max_val=E - 1)
            gain_and_shift(0, 0, lambda s, k: e0)

            def step(s, k, rounds, expert_of):
                if real(s):
                    expert_of(s + 1, k + 1)
                    layernorm_1(s + 2, k + 2, rounds)
                if real(s - 3):
                    act.wait_ge(z_ok, s - 2)
                    a.activation(sg[:, k % RB, :], y[:, k % RB, :], ACT.Sigmoid).then_inc(sg_ok, 1)
                if real(s):
                    gain_and_shift(s + 1, k + 1, expert_of)
                if real(s - 1):
                    act.wait_ge(hT_ps_ok, s)
                    a.activation(hT[:, (k - 1) % RB, :, :].rearrange("p c t -> p (c t)"), hT_ps[(k - 1) % RB],
                                 ACT.Relu).then_inc(hT_ok, 1)
                if real(s):
                    layernorm_2(s + 2, k + 2)
            slot_steps(act, step)

        @block.tensor
        def _(pe):
            t = nc.tensor
            pe.wait_ge(const_ok, 1)
            pe.wait_ge(small_in, 64)
            t.transpose(small_ps, small[:, :], ident[0:3 * E, 0:3 * E]).then_inc(small_T, 1)
            pe.wait_ge(small_ok, 1)
            pe.wait_ge(w_in, 64)

            with pe.Fori(0, SEQS) as b:
                pe.wait_ge(xs_ok, b + 1)
                pe.wait_ge(pj_ok, b * TPS + 1)
                for j in range(TPS + 1):
                    if j < TPS:
                        t.transpose(bank[:, 4 + j % 2, 0:P], xs[:, j, :], ident[:, :]).then_inc(xT_ps_ok, 1)
                    if j:
                        pe.wait_ge(xT_ok, b * TPS + j)
                        t.matmul(bank[:, j - 1, 0:PW], xT[:, (j - 1) % 2, :], wcat[:, :], start=True,
                                 stop=True).then_inc(pj_ps_ok, 1)

            pe.wait_ge(oh_ok, 1)
            oh2 = oh[:, :, :].rearrange("p n e -> p (n e)")
            t.matmul(rank_ps, before[:, :], oh2, start=True, stop=False)
            for back in range(1, NT):
                t.matmul(rank_ps[:, back * E:], ones[:, :], oh2[:, 0:(NT - back) * E], start=False, stop=(back == NT - 1))
            for n in range(NT):
                last = t.matmul(total_ps, ones[:, :], oh[:, n, :], start=(n == 0), stop=(n == NT - 1))
            last.then_inc(rank_ok, 1)
            pe.wait_ge(oneh_ok, 1)
            for n in range(NT):
                last = t.matmul(inv_ps, ohb[:, n, :], oha[:, n, :, :].rearrange("p a s -> p (a s)"),
                                start=(n == 0), stop=(n == NT - 1))
            last.then_inc(inv_ok, 1)
            pe.wait_ge(idx_ok, 1)
            pe.wait_ge(wo_in, 16)
            pe.sem_inc(pre_ok, 2)

            def turn_output(b, j):
                n = b * TPS + j
                pe.wait_ge(red_ok, n + 2)
                if not isinstance(n, int) or n:
                    pe.wait_ge(aT_ok, n)
                if j == 0:
                    t.transpose(aT_ps, attn[:, j % 2, :], ident[:, :]).then_inc(aT_ps_ok, 1)
                else:
                    t.matmul(aT_ps, attn[:, j % 2, :], ident[:, :], start=True, stop=False)
                    pe.wait_ge(qT_ok, b * (TPS - 1) + j)
                    pe.wait_ge(st_ok, b * (TPS - 1) + j)
                    t.matmul(aT_ps, state[:, j - 1, :], qT[:, j % 2, :], start=False, stop=True).then_inc(aT_ps_ok, 1)

            def output_product(b, j):
                n = b * TPS + j
                pe.wait_ge(aT_ok, n + 1)
                if not isinstance(n, int) or n:
                    pe.wait_ge(s_ok, n)
                t.matmul(s_ps, aT[:, j % 2, :], wo_sb[:, :], start=True, stop=True).then_inc(s_ps_ok, 1)

            def tiles(b, first):
                for j in range(TPS):
                    n = b * TPS + j

                    def sums(half):
                        return t.matmul(prefix[:, j % 2, half * BANK:(half + 1) * BANK], tri[:, :],
                                        kv[:, j % 2, half * BANK:(half + 1) * BANK], start=True, stop=True)
                    pe.wait_ge(kv_ok, n + 1)
                    pe.wait_ge(m_ok, n + 1)
                    sums(0)
                    pe.wait_ge(qk_ok, n + 1)
                    if j:
                        if j > 1 or not first:
                            pe.wait_ge(qT_ok, b * (TPS - 1) + j - 1)
                        t.transpose(qT_ps, qk[:, j % 2, 0:D], ident[:, :]).then_inc(qT_ps_ok, 1)
                    if j < TPS - 1:
                        if j or not first:
                            pe.wait_ge(st_ok, b * (TPS - 1) + j)
                        t.matmul(st_ps, qk[:, j % 2, D:2 * D],
                                 proj[:, bass.ds(n, 1), CV:CV + D].rearrange("p o c -> p (o c)"), start=(j == 0), stop=True,
                                 skip_group_check=True).then_inc(st_ps_ok, 1)
                    sums(1).then_inc(pre_ok, 1)
                    if j or not first:
                        turn_output(*((b, j - 1) if j else (b - 1, TPS - 1)))
                    if j >= 2 or not first:
                        output_product(*((b, j - 2) if j >= 2 else (b - 1, TPS - 2 + j)))
            tiles(0, True)
            with pe.Fori(1, SEQS) as b:
                tiles(b, False)
            turn_output(SEQS - 1, TPS - 1)
            output_product(SEQS - 1, TPS - 2)
            output_product(SEQS - 1, TPS - 1)

            pe.wait_ge(ffn_in, 64)

            def transpose_x(s, k):
                pe.wait_ge(xl_ok, s + 1)
                t.transpose(xlT_ps, xl[:, k % RB, :], ident[:, :]).then_inc(xlT_ps_ok, 1)
            transpose_x(0, 0)

            def step(s, k, rounds, expert_of):
                if real(s):
                    e = expert_of(s, k)
                    pe.wait_ge(xlT_ok, s + 1)
                    t.matmul(h_ps[k % RB], xlT[:, k % RB, :],
                             w1_sb[:, bass.ds(e, 1), :].rearrange("p o f -> p (o f)"), start=True,
                             stop=True).then_inc(h_ps_ok, 1)
                    if real(s + 1) and k < FIRST + RG - 1:
                        expert_of(s + 1, k + 1)
                    transpose_x(s + 1, k + 1)
                if real(s - 1):
                    r = (k - 1) % RB
                    pe.wait_ge(h_ok, s)
                    for c in range(FC):
                        last = t.transpose(hT_ps[r][:, c * P:c * P + P], h[:, r, c * P:c * P + P], ident[:, :])
                    last.then_inc(hT_ps_ok, 1)
                if real(s - 2):
                    r = (k - 2) % RB
                    e = expert_of(s - 2, k - 2)
                    pe.wait_ge(hT_ok, s - 1)
                    if real(s - 3):
                        pe.wait_ge(y1_ok, s - 2)
                    for c in range(FC):
                        last = t.matmul(y_ps, hT[:, r, c, :],
                                        w2_sb[:, bass.ds(e, 1), c, :].rearrange("p o d -> p (o d)"),
                                        start=(c == 0), stop=(c == FC - 1))
                    last.then_inc(y_ps_ok, 1)
            slot_steps(pe, step)

        @block.vector
        def _(dve):
            v = nc.vector
            chain = [0]

            def link(ins):
                chain[0] += 1
                ins.then_inc(dv, 1)
                dve.wait_ge(dv, chain[0])

            dve.wait_ge(iota_ok, 1)
            v.memset(ones[:, :], 1.0)
            for z in pe8:
                v.memset(z[:, :], 0.0)
            link(v.tensor_single_scalar(phead_i[:, :], pidx_i[:, :], 3, ALU.arith_shift_right))
            v.tensor_scalar(tri[:, :], col[:, :], pidx[:, 0:1], None, ALU.is_ge)
            v.tensor_scalar(before[:, :], col[:, :], pidx[:, 0:1], None, ALU.is_gt)
            v.tensor_scalar(ident[:, :], col[:, :], pidx[:, 0:1], None, ALU.is_equal).then_inc(const_ok, 1)
            link(v.tensor_copy(phead[:, :], phead_i[:, :]))
            v.tensor_scalar(same_head[:, :], colhead[:, :, :].rearrange("p h d -> p (h d)"), phead[:, 0:1], None, ALU.is_equal)
            dve.sem_inc(sum_ok, 1)

            def mean_and_variance(st, mean, var):
                v.tensor_tensor(mean, st[:, :, 1], st[:, :, 4], ALU.add)
                v.tensor_tensor(tmp[:, :], st[:, :, 1], st[:, :, 4], ALU.subtract)
                link(v.tensor_tensor(var, st[:, :, 2], st[:, :, 5], ALU.add))
                v.tensor_scalar(mean, mean, 0.5, None, ALU.mult)
                v.scalar_tensor_tensor(tmp[:, :], tmp[:, :], 0.25, tmp[:, :], ALU.mult, ALU.mult)
                link(v.tensor_scalar(var, var, 1.0 / D, LN_EPS, ALU.mult, ALU.add))
                return v.tensor_tensor(var, var, tmp[:, :], ALU.add)

            def newton(r, a_, t_):
                link(v.tensor_tensor(t_, r, r, ALU.mult))
                link(v.scalar_tensor_tensor(t_, t_, -0.5, a_, ALU.mult, ALU.mult))
                return v.scalar_tensor_tensor(r, t_, 1.5, r, ALU.add, ALU.mult)

            for b in range(SEQS):
                dve.wait_ge(x_in[b], 16)
                for n in range(b * TPS, b * TPS + TPS):
                    last = v.bn_stats(st1[:, n, :], row[:, n, RX:RX + D])
            link(last)
            mean_and_variance(st1, mean1[:, :], var1[:, :]).then_inc(var1_ok, 1)
            dve.wait_ge(sqrt1_ok, 2)
            link(newton(row[:, :, RSC1], var1[:, :], tmp[:, :]))
            link(v.scalar_tensor_tensor(row[:, :, RSH1], mean1[:, :], -1.0, row[:, :, RSC1], ALU.mult, ALU.mult))

            def xn_of(b):
                for j in range(TPS):
                    n = b * TPS + j
                    r = row[:, bass.ds(n, 1), :].rearrange("p o c -> p (o c)")
                    last = v.tensor_scalar(xs[:, j, :], r[:, RX:RX + D], r[:, RSC1:RSC1 + 1], r[:, RSH1:RSH1 + 1],
                                           ALU.mult, ALU.add)
                last.then_inc(xs_ok, 1)
                dve.wait_ge(xs_ok, b + 1)
                for j in range(TPS):
                    last = v.bn_stats(st2[:, bass.ds(b * TPS + j, 1), :].rearrange("p o c -> p (o c)"), xs[:, j, :])
                last.then_inc(st2_ok, 1)

            def squared_norms(b):
                dve.wait_ge(sq_ok, b + 2)
                v.tensor_reduce(ss[:, bass.ds(b * TPS, TPS), :, :].rearrange("p j a h -> p j (a h)"),
                                sq.rearrange("p j (h d) -> p j h d", d=DH), AX.X, ALU.add).then_inc(sum_ok, 1)
                dve.wait_ge(sum_ok, b + 2)
                s4 = ss[:, bass.ds(b * TPS, TPS), :, :].rearrange("p j a h -> p j (a h)")
                v.tensor_scalar(s4, s4, NORM_EPS2, None, ALU.max).then_inc(ss_ok, 1)

            xn_of(0)
            with dve.Fori(1, SEQS) as b:
                dve.wait_ge(xT_ps_ok, b * TPS)
                dve.wait_ge(st2_ok, b)
                xn_of(b)
                squared_norms(b - 1)
            squared_norms(SEQS - 1)

            dve.wait_ge(pj_ok, NT + 1)
            aff = proj[:, :, CA:CA + E]

            def over_tiles(ap):
                return ap.unsqueeze(1).to_broadcast([P, NT, E])

            def over_experts(ap):
                return ap.unsqueeze(2).to_broadcast([P, NT, E])

            v.tensor_reduce(mx[:, :], aff, AX.X, ALU.max).then_inc(mx_ok, 1)
            v.tensor_tensor(logit, proj[:, :, CB:CB + H], bb_bc[:, :].unsqueeze(1).to_broadcast([P, NT, H]),
                            ALU.add).then_inc(logit_ok, 1)
            dve.wait_ge(mx_ok, 1)
            link(v.tensor_tensor(eq, aff, over_experts(mx[:, :]), ALU.is_equal))
            link(v.tensor_tensor(eq, eq, over_tiles(rev[:, :]), ALU.mult))
            link(v.tensor_reduce(mw[:, :], eq, AX.X, ALU.max))
            v.tensor_tensor(oh[:, :, :], eq, over_experts(mw[:, :]), ALU.is_equal).then_inc(oh_ok, 1)
            dve.wait_ge(st2_ok, SEQS)
            mean_and_variance(st2, mean2[:, :], var2[:, :]).then_inc(ln2_ok, 1)
            dve.wait_ge(lnk_ok, 3)
            link(newton(rnorm[:, :, 1, :], ss[:, :, 1, :], tmp_n[:, :, 1, :]))
            dve.wait_ge(sig_ok, 1)
            v.tensor_tensor(rnorm[:, :, 1, :], rnorm[:, :, 1, :], logit, ALU.mult).then_inc(bvs_ok, 1)
            dve.wait_ge(r2_ok, 2)
            link(newton(row[:, :, RSC2], var2[:, :], tmp[:, :]))
            v.scalar_tensor_tensor(row[:, :, RSH2], mean2[:, :], -1.0, row[:, :, RSC2], ALU.mult, ALU.mult).then_inc(scalars_ok, 1)
            dve.wait_ge(rank_ok, 1)
            link(v.tensor_copy(pos[:, 0:E], total_ps))
            link(v.tensor_tensor(cmp, pos[:, 0:E].unsqueeze(2).to_broadcast([P, E, NT]),
                                 steps[:, :].unsqueeze(1).to_broadcast([P, E, NT]), ALU.is_gt))
            link(v.tensor_reduce(pe8[0][:, 4:], cmp, AX.X, ALU.add))
            es = 0
            for shift in (1, 2, 4):
                link(v.tensor_tensor(pe8[1 - es][:, 4:], pe8[es][:, 4:], pe8[es][:, 4 - shift:4 + E - shift], ALU.add))
                es = 1 - es
            link(v.scalar_tensor_tensor(eq, over_tiles(pe8[es][:, 3:3 + E]), float(P),
                                        rank_ps.rearrange("p (n e) -> p n e", e=E), ALU.mult, ALU.add))
            link(v.tensor_tensor(eq, eq, oh[:, :, :], ALU.mult))
            link(v.tensor_reduce(pos[:, :], eq, AX.X, ALU.add))
            link(v.tensor_copy(pos_i[:, :], pos[:, :]))
            v.tensor_single_scalar(pa_i[:, :], pos_i[:, :], 7, ALU.arith_shift_right)
            link(v.tensor_single_scalar(pb_i[:, :], pos_i[:, :], P - 1, ALU.bitwise_and))
            v.tensor_copy(pa[:, :], pa_i[:, :])
            link(v.tensor_copy(pb[:, :], pb_i[:, :]))
            valid = oha[:, :, 2, :]
            v.tensor_tensor(valid, slotno[:, :].unsqueeze(1).to_broadcast([P, NT, ALL]),
                            pa[:, :].unsqueeze(2).to_broadcast([P, NT, ALL]), ALU.is_equal)
            link(v.tensor_tensor(ohb, col[:, :].unsqueeze(1).to_broadcast([P, NT, P]),
                                 pb[:, :].unsqueeze(2).to_broadcast([P, NT, P]), ALU.is_equal))
            v.tensor_scalar(oha[:, :, 0, :], valid, pidx[:, 0:1], None, ALU.mult)
            v.tensor_tensor(oha[:, :, 1, :], valid, tileno[:, :].unsqueeze(2).to_broadcast([P, NT, ALL]),
                            ALU.mult).then_inc(oneh_ok, 1)
            link(v.tensor_tensor(scmp[:, :, :], slotno[0:1, :].unsqueeze(2).to_broadcast([1, ALL, E - 1]),
                                 pe8[es][0:1, 4:4 + E - 1].unsqueeze(1).to_broadcast([1, ALL, E - 1]), ALU.is_ge))
            link(v.tensor_reduce(sexp[:, :], scmp[:, :, :], AX.X, ALU.add))
            v.tensor_copy(sexp_i[:, :], sexp[:, :])
            dve.wait_ge(inv_ok, 1)
            link(v.tensor_copy(inv[:, :, :].rearrange("p a s -> p (a s)"), inv_ps))
            v.scalar_tensor_tensor(tok[:, :], inv[:, 1, :], float(P), inv[:, 0, :], ALU.mult, ALU.add)
            link(v.tensor_scalar(past[:, :], inv[:, 2, :], -NOWHERE, NOWHERE, ALU.mult, ALU.add))
            link(v.tensor_tensor(past[:, :], past[:, :], tok[:, :], ALU.add))
            v.tensor_copy(gidx[:, :], tok[:, :])
            v.tensor_copy(sidx[:, :], past[:, :]).then_inc(idx_ok, 1)

            dve.sem_inc(m_ok, 2)
            dve.sem_inc(red_ok, 1)
            dve.wait_ge(qn_ok, 1)

            def tiles(b):
                for j in range(TPS):
                    n = b * TPS + j
                    q3 = proj[:, bass.ds(n, 1), CQ:CQ + D].rearrange("p o (h d) -> p (o d) h", d=DH)
                    if j == 0:
                        dve.wait_ge(qn_ok, b + 1)
                    dve.wait_ge(red_ok, n + 1)
                    dve.wait_ge(pre_ok, n + 3)
                    v.tensor_tensor(m[:, :].rearrange("p (d h e) -> p d h e", d=DH, h=H),
                                    prefix[:, j % 2, :].rearrange("p (d h e) -> p d h e", d=DH, h=H),
                                    q3.unsqueeze(3).to_broadcast([P, DH, H, DH]), ALU.mult).then_inc(m_ok, 1)
                    if j < TPS - 1:
                        dve.wait_ge(st_ps_ok, b * (TPS - 1) + j + 1)
                        v.tensor_tensor(state[:, j, :], st_ps, same_head[:, :], ALU.mult).then_inc(st_ok, 1)
                    dve.wait_ge(m_ok, n + 3)
                    v.tensor_reduce(attn[:, j % 2, :], m[:, :].rearrange("p (d c) -> p c d", d=DH), AX.X,
                                    ALU.add).then_inc(red_ok, 1)
            with dve.Fori(0, SEQS) as b:
                tiles(b)

            dve.wait_ge(ffn_in, 64)

            def step(s, k, rounds, expert_of):
                a, ra, ga = real(s - 3), k % RB, (k - 3) % RG
                if a:
                    e = expert_of(s - 3, k - 3)
                    dve.wait_ge(y_ps_ok, s - 2)
                    v.tensor_tensor(y[:, ra, :], y_ps, b2_bc[:, bass.ds(e, 1), :].rearrange("p o d -> p (o d)"),
                                    ALU.add).then_inc(y1_ok, 1)
                    dve.wait_ge(y1_ok, s - 2)
                    v.scalar_tensor_tensor(y[:, ra, :], y[:, ra, :], rg[:, ga, RALPHA:RALPHA + 1], xn[:, ga, :],
                                           ALU.mult, ALU.add).then_inc(z_ok, 1)
                if real(s):
                    e = expert_of(s, k)
                    dve.wait_ge(h_ps_ok, s + 1)
                    v.tensor_tensor(h[:, ra, :], h_ps[ra], b1_bc[:, bass.ds(e, 1), :].rearrange("p o f -> p (o f)"),
                                    ALU.add).then_inc(h_ok, 1)
                    if real(s + 1) and k < FIRST + RG - 1:
                        expert_of(s + 1, k + 1)
                if a:
                    dve.wait_ge(z_ok, s - 2)
                    v.tensor_tensor(u[:, ra, :], y[:, ra, :], rg[:, ga, RS:RS + D], ALU.mult).then_inc(u_ok, 1)
                    dve.wait_ge(sg_ok, s - 2)
                    dve.wait_ge(u_ok, s - 2)
                    v.tensor_tensor(u[:, ra, :], u[:, ra, :], sg[:, ra, :], ALU.mult).then_inc(y2_ok, 1)
                    dve.wait_ge(y2_ok, s - 2)
                    dve.wait_ge(o_free, s - 2)
                    v.tensor_tensor(o[:, ra, :], u[:, ra, :], rg[:, ga, RX:RX + D], ALU.add).then_inc(o_ok, 1)
            slot_steps(dve, step)


_INS = ["L0_attn_x", "L0_attn_Wq", "L0_attn_Wk", "L0_attn_Wv", "L0_attn_Wo", "L0_attn_Wb", "L0_attn_bb",
        "L0_ffn_centroids", "L0_ffn_ln_g", "L0_ffn_ln_b", "L0_ffn_w1", "L0_ffn_b1", "L0_ffn_w2", "L0_ffn_b2"]


def kernel(**inputs):
    import numpy as _np
    import concourse.bacc as _bacc
    from concourse.bass_utils import run_bass_kernel_spmd as _run

    nc = _bacc.Bacc("TRN2", target_bir_lowering=False, num_devices=1)
    arrays, args = {}, []
    for name in _INS:
        a = _np.ascontiguousarray(inputs[name])
        arrays[f"in_{name}"] = a
        args.append(nc.dram_tensor(f"in_{name}", a.shape, mybir.dt.from_np(a.dtype), kind="ExternalInput").ap())
    args.append(nc.dram_tensor("out_dram", (SEQS, SEQ, D), F32, kind="ExternalOutput").ap())
    build(nc, *args)
    r = _run(nc, [arrays], core_ids=[0])
    return r.results[0]["out_dram"]
```

```python
from contextlib import ExitStack

import concourse.bass as bass
from concourse import mybir

F32 = mybir.dt.float32
BF16 = mybir.dt.bfloat16
I32 = mybir.dt.int32
ALU = mybir.AluOpType
ACT = mybir.ActivationFunctionType
AX = mybir.AxisListType

P = 128
D = 128
H, DH = 16, 8
SEQS, SEQ = 8, 512
NT = SEQS * SEQ // P
TPS = SEQ // P
E, F = 8, 512
FC = F // P
TOKENS = NT * P
SLOTS = NT + E - 1
KVW = DH * H * DH
BANK = 512
CQ, CK, CV, CB, CA = 0, D, 2 * D, 3 * D, 3 * D + H
PW = CA + E
RX, RALPHA, RSC1, RSH1, RSC2, RSH2, RS = 0, D, D + 1, D + 2, D + 3, D + 4, D + 5
HALF_ROW = RS
RW = 2 * HALF_ROW
LN_EPS = 1e-5
NORM_EPS2 = 1e-24
NOWHERE = 8192.0
RB = 3
RG = 12
RO = RG
UNDER_WAY = 4
EARLY = 6
FIRST = 3
ROUNDS = (SLOTS - FIRST) // RG - 1


def build(nc, x, wq, wk, wv, wo, wb, bb, cent, ln_g, ln_b, w1, b1, w2, b2, out):
    rows_dram = nc.dram_tensor("token_rows", (TOKENS, RW), F32).ap()
    first_dram = nc.dram_tensor("token_rows_first_units", (TOKENS, HALF_ROW), F32).ap()
    xt = x.rearrange("s (j p) d -> p (s j) d", p=P)
    out_rows = out.rearrange("s l d -> (s l) d")
    ctx = ExitStack()
    with ctx:
        def sb(name, shape, dt=F32):
            return ctx.enter_context(nc.sbuf_tensor(name, shape, dt))

        def sem(name):
            return ctx.enter_context(nc.semaphore(name))

        row = sb("row", [P, NT, RW])
        proj = sb("proj", [P, NT, PW])
        wcat = sb("wcat", [D, PW])
        wo_sb = sb("wo_sb", [D, D])
        small = sb("small", [(3 + FC) * E, D])
        gb = sb("gb", [D, 2 * E])
        bb_bc = sb("bb_bc", [P, H])
        w1_sb = sb("w1_sb", [D, E, F])
        w2_sb = sb("w2_sb", [P, E, FC, D])
        b1_sb = sb("b1_sb", [P, E, FC])
        b2_sb = sb("b2_sb", [1, E, D])
        w1s = [sb(f"w1s{i}", [D, F]) for i in range(2)]
        ones_row = sb("ones_row", [1, P])
        col = sb("col", [P, D])
        colhead = sb("colhead", [P, H, DH])
        pidx = sb("pidx", [P, 1])
        pidx_i = sb("pidx_i", [P, 1], I32)
        phead_i = sb("phead_i", [P, 1], I32)
        phead = sb("phead", [P, 1])
        pplus = sb("pplus", [P, 1])
        rev = sb("rev", [P, E])
        steps = sb("steps", [P, NT])
        tileno = sb("tileno", [P, NT])
        slotno = sb("slotno", [P, SLOTS])
        ident = sb("ident", [P, P])
        tri = sb("tri", [P, P])
        before = sb("before", [P, P], BF16)
        ones = sb("ones", [P, P], BF16)
        same_head = sb("same_head", [P, P])
        st1 = sb("st1", [P, NT, 6])
        st2 = sb("st2", [P, NT, 6])
        mean1 = sb("mean1", [P, NT])
        var1 = sb("var1", [P, NT])
        mean2 = sb("mean2", [P, NT])
        var2 = sb("var2", [P, NT])
        tmp = sb("tmp", [P, NT])
        kv = sb("kv", [P, 2, KVW])
        xs = [sb("xs", [P, TPS, D]), kv[:, 0, 0:TPS * D].rearrange("p (j c) -> p j c", j=TPS)]
        qk = xs[0][:, :, :].rearrange("p (i a) c -> p i (a c)", i=2)
        xT = sb("xT", [D, TPS, P])
        m = sb("m", [P, KVW])
        sq = [z.rearrange("p (j c) -> p j c", j=TPS) for z in (m[:, :], kv[:, 1, :])]
        ss = sb("ss", [P, NT, 2, H])
        rnorm = sb("rnorm", [P, NT, 2, H])
        mx = sb("mx", [P, NT])
        mw = sb("mw", [P, NT])
        oh_all = sb("oh", [P, NT + 1, E], BF16)
        oh = oh_all[:, 0:NT, :]
        pe8 = [sb(f"pe8{i}", [P, 4 + E]) for i in range(2)]
        pos = sb("pos", [P, NT])
        pos_i = sb("pos_i", [P, NT], I32)
        pa_i = sb("pa_i", [P, NT], I32)
        pb_i = sb("pb_i", [P, NT], I32)
        pa = sb("pa", [P, NT])
        pb = sb("pb", [P, NT])
        inv = sb("inv", [P, 2, SLOTS])
        nothing = sb("nothing", [P, SLOTS])
        tok = sb("tok", [P, SLOTS])
        past = sb("past", [P, SLOTS])
        gidx = sb("gidx", [P, SLOTS], I32)
        uidx = sb("uidx", [P, EARLY], I32)
        sidx = sb("sidx", [P, SLOTS], I32)
        scmp = sb("scmp", [1, SLOTS, E - 1])
        sexp = sb("sexp", [1, SLOTS])
        sexp_i = sb("sexp_i", [1, SLOTS], I32)
        WORK = max(RB * (F + 4 * D) + RO * D, NT * (3 * H + 2 * E + P // 2) + NT * 3 * SLOTS // 2)
        work = sb("work", [P, WORK])
        used = [0]

        def part(words):
            used[0] += words
            assert used[0] <= WORK
            return work[:, used[0] - words:used[0]]

        logit = part(NT * H).rearrange("p (n h) -> p n h", n=NT)
        tmp_n = part(NT * 2 * H).rearrange("p (n a h) -> p n a h", n=NT, a=2)
        eq = part(NT * E).rearrange("p (n e) -> p n e", n=NT)
        cmp = part(NT * E).rearrange("p (e n) -> p e n", e=E)
        ohb = part(NT * P // 2).bitcast(BF16).rearrange("p (n c) -> p n c", n=NT)
        oha = part(NT * 3 * SLOTS // 2).bitcast(BF16).rearrange("p (a n s) -> p a n s", n=NT, a=3)
        apart = tmp_n[:, 0:P // (2 * H), :, :].rearrange("p n a h -> p (n a h)")
        attn = sb("attn", [P, 2, D])
        state = sb("state", [P, TPS - 1, D])
        qT = sb("qT", [P, 2, P])
        aT = xT
        rg = proj
        used[0] = 0
        xl, xlT, y, sg = (part(RB * D).rearrange("p (r c) -> p r c", r=RB) for _ in range(4))
        o = part(RO * D).rearrange("p (r c) -> p r c", r=RO)
        hT = part(RB * F).rearrange("p (r c t) -> p r c t", r=RB, c=FC)
        xn = proj[:, RG:2 * RG, 0:D]
        u = kv[:, 0, 0:RB * D].rearrange("p (r c) -> p r c", r=RB)

        bank = ctx.enter_context(nc.psum_tensor("bank", [P, 8, BANK], F32))
        prefix = bank[:, 0:4, :].rearrange("p (i a) c -> p i (a c)", i=2)
        small_ps = bank[:, 6, 0:(3 + FC) * E]
        ranks_ps = bank[:, 6, 0:(NT + 1) * E]
        rank_ps, total_ps = ranks_ps[:, 0:NT * E], ranks_ps[:, NT * E:]
        inv_ps = bank[:, 7, 0:2 * SLOTS]
        st_ps = bank[:, 4, 0:D]
        qT_ps = bank[:, 5, 0:P]
        aT_ps = bank[:, 6, 0:P]
        s_ps = bank[:, 7, 0:D]
        hT_ps = [bank[:, i, :] for i in (0, 1)]
        xlT_ps = bank[:, 5, 0:P]
        y_ps = [bank[:, i, 0:D] for i in (6, 7)]

        names = """w_in small_in bb_in wo_in ffn_in iota_ok const_ok small_T small_ok dv
            var1_ok sqrt1_ok scale1_ok xs_ok xs_act_ok st2_ok xT_ps_ok xT_ok pj_ps_ok pj_ok sq_ok
            sum_ok ss_ok ln2_ok logit_ok lnk_ok lnq_ok r2_ok sig_ok mx_ok alpha_ok pl bvs_ok q_scale_ok scalars_ok
            oh_ok rank_ok digits_ok valid_ok oneh_ok apart_ok ohb_ok inv_ok inv_read idx_ok
            bv_ok qn_ok kv_ok pre_ok m_ok red_ok qk_ok qT_ps_ok qT_ok st_ps_ok st_ok aT_ps_ok aT_ok s_ps_ok s_ok rows_x_out rows_out
            xn_ok xl_ok xlT_ps_ok xlT_ok w1_ok hT_ps_ok b1_ok hT_ok y_ps_ok z_ok u_ok sg_ok y2_ok o_ok o_free"""
        S = {n: sem(n) for n in names.split()}
        (w_in, small_in, bb_in, wo_in, ffn_in, iota_ok, const_ok, small_T, small_ok, dv,
         var1_ok, sqrt1_ok, scale1_ok, xs_ok, xs_act_ok, st2_ok, xT_ps_ok, xT_ok, pj_ps_ok, pj_ok, sq_ok,
         sum_ok, ss_ok, ln2_ok, logit_ok, lnk_ok, lnq_ok, r2_ok, sig_ok, mx_ok, alpha_ok, pl, bvs_ok, q_scale_ok, scalars_ok,
         oh_ok, rank_ok, digits_ok, valid_ok, oneh_ok, apart_ok, ohb_ok, inv_ok, inv_read, idx_ok,
         bv_ok, qn_ok, kv_ok, pre_ok, m_ok, red_ok, qk_ok, qT_ps_ok, qT_ok, st_ps_ok, st_ok, aT_ps_ok, aT_ok, s_ps_ok,
         s_ok, rows_x_out, rows_out,
         xn_ok, xl_ok, xlT_ps_ok, xlT_ok, w1_ok, hT_ps_ok, b1_ok, hT_ok, y_ps_ok, z_ok, u_ok, sg_ok, y2_ok,
         o_ok, o_free) = S.values()
        x_in = [sem(f"x_in{i}") for i in range(SEQS // 2)]
        gath = [sem(f"gath{i}") for i in range(RG)]
        scat = [sem(f"scat{i}") for i in range(RO)]

        def real(s):
            return not isinstance(s, int) or 0 <= s < SLOTS

        def ahead(eng, *values):
            return [v if isinstance(v, int) else eng.snap(v) for v in values]

        def slot_steps(eng, step, keep, ahead_by):
            known = {}

            def expert_of(s, k):
                if k not in known:
                    at = sexp_i[0:1, s:s + 1] if isinstance(s, int) else sexp_i[0:1, bass.ds(s, 1)]
                    known[k] = eng.value_load(at, min_val=0, max_val=E - 1)
                return known[k]
            for s in range(FIRST):
                step(s, s, 0, expert_of)
            carried = {k: eng.alloc_register(f"expert_{k}") for k in range(FIRST - keep, FIRST + ahead_by)}
            for k, reg in carried.items():
                eng.reg_mov(reg, expert_of(k, k))
            with eng.Fori(0, ROUNDS) as it:
                known.clear()
                for k, reg in carried.items():
                    known[k] = eng.snap(reg, min_val=0, max_val=E - 1)
                for k in range(FIRST, FIRST + RG):
                    step(it * RG + k, k, it, expert_of)
                for k, reg in carried.items():
                    eng.reg_mov(reg, expert_of(it * RG + k + RG, k + RG))
            known.clear()
            for k, reg in carried.items():
                known[ROUNDS * RG + k] = eng.snap(reg, min_val=0, max_val=E - 1)
            for s in range(FIRST + ROUNDS * RG, SLOTS + 2):
                step(s, s, 0, expert_of)

        halves = slice(0, NT // 2), slice(NT // 2, NT)

        block = ctx.enter_context(nc.Block())

        @block.sync
        def _(sp):
            for i in range(SEQS // 2):
                two = slice(i * 2 * TPS, (i + 1) * 2 * TPS)
                sp.dma_start(row[:, two, RX:RX + D], xt[:, two, :]).then_inc(x_in[i], 16)
            sp.dma_start(bb_bc[:, :], bb.partition_broadcast(P)).then_inc(bb_in, 16)
            sp.wait_ge(w_in, 64)
            sp.dma_start(wo_sb[:, :], wo).then_inc(wo_in, 16)
            sp.dma_start(w1_sb[:, :, :], w1.rearrange("e d f -> d e f")).then_inc(ffn_in, 16)
            sp.dma_start(w2_sb[:, :, :, :], w2.rearrange("e (c p) d -> p e c d", p=P)).then_inc(ffn_in, 16)
            sp.dma_start(b2_sb[:, :, :], b2.unsqueeze(0)).then_inc(ffn_in, 16)
            sp.wait_ge(alpha_ok, 1)
            sp.wait_ge(scalars_ok, 1)
            sp.dma_start(first_dram.rearrange("(n p) c -> p n c", p=P), row[:, :, 0:RS]).then_inc(rows_x_out, 16)

            def rows_of(n, tiles):
                sp.wait_ge(s_ok, n + tiles)
                sp.dma_start(rows_dram[bass.ds(n * P, tiles * P), :].rearrange("(j p) c -> p j c", p=P),
                             row[:, bass.ds(n, tiles), :]).then_inc(rows_out, 16)
            with sp.Fori(0, SEQS - 1) as b:
                rows_of(b * TPS, TPS)
            rows_of(NT - TPS, TPS - 2)
            rows_of(NT - 2, 2)

        @block.gpsimd
        def _(pool):
            g = nc.gpsimd

            def iota(ap, pattern, base=0, per_partition=0):
                return g.iota(ap, pattern, base=base, channel_multiplier=per_partition, allow_small_or_imprecise_dtypes=True)
            iota(pidx_i[:, :], [[0, 1]], per_partition=1)
            iota(col[:, :], [[1, D]])
            iota(pidx[:, :], [[0, 1]], per_partition=1)
            iota(pplus[:, :], [[0, 1]], base=1, per_partition=1)
            iota(colhead[:, :, :], [[1, H], [0, DH]])
            iota(rev[:, :], [[-1, E]], base=E)
            iota(steps[:, :], [[P, NT]])
            iota(tileno[:, :], [[1, NT]])
            iota(slotno[:, :], [[1, SLOTS]]).then_inc(iota_ok, 1)
            def squares(b, i, width):
                pool.wait_ge(pj_ok, b * TPS + TPS + TPS)
                pool.wait_ge(sum_ok, b + 1)
                p4 = proj[:, bass.ds(b * TPS, TPS), CQ:CQ + width]
                g.tensor_tensor(sq[i][:, :, 0:width], p4, p4, ALU.mult).then_inc(sq_ok, 1)
            with pool.Fori(0, SEQS // 2 - 1) as pair:
                for i in range(2):
                    squares(pair * 2 + i, i, 2 * D)
            squares(SEQS - 2, 0, 2 * D)
            squares(SEQS - 1, 1, D)
            pool.wait_ge(bb_in, 16)
            g.tensor_tensor(logit, proj[:, :, CB:CB + H], bb_bc[:, :].unsqueeze(1).to_broadcast([P, NT, H]),
                            ALU.add).then_inc(logit_ok, 1)
            pool.wait_ge(lnq_ok, 3)
            a_q, r_q, t_q = ss[:, :, 0, :], rnorm[:, :, 0, :], tmp_n[:, :, 0, :]
            g.tensor_tensor(t_q, t_q, a_q, ALU.mult).then_inc(pl, 1)
            pool.wait_ge(pl, 1)
            g.tensor_scalar(t_q, t_q, -0.5, 1.5, ALU.mult, ALU.add).then_inc(pl, 1)
            pool.wait_ge(pl, 2)
            g.tensor_tensor(r_q, r_q, t_q, ALU.mult).then_inc(q_scale_ok, 1)
            pool.wait_ge(q_scale_ok, 1)

            def scale_values(b):
                v4 = proj[:, bass.ds(b * TPS, TPS), CV:CV + D].rearrange("p j (h e) -> p j h e", e=DH)
                g.tensor_tensor(v4, v4, rnorm[:, bass.ds(b * TPS, TPS), 1, :].unsqueeze(3).to_broadcast([P, TPS, H, DH]),
                                ALU.mult).then_inc(bv_ok, 1)

            def norm_queries(b):
                q4 = proj[:, bass.ds(b * TPS, TPS), CQ:CQ + D].rearrange("p j (h d) -> p j h d", d=DH)
                g.tensor_tensor(q4, q4, rnorm[:, bass.ds(b * TPS, TPS), 0, :].unsqueeze(3).to_broadcast([P, TPS, H, DH]),
                                ALU.mult).then_inc(qn_ok, 1)

            def outer_products(b, first, more):
                read = ahead(pool, *(b * TPS + j - 1 for j in range(TPS)))
                pool.wait_ge(bv_ok, b + 1)
                for j in range(TPS):
                    n = b * TPS + j
                    if j >= 2 or not first:
                        pool.wait_ge(pre_ok, read[j])
                    k3 = proj[:, bass.ds(n, 1), CK:CK + D].rearrange("p o (h d) -> p (o d) h", d=DH)
                    v3 = proj[:, bass.ds(n, 1), CV:CV + D].rearrange("p o (h e) -> p (o h) e", e=DH)
                    g.tensor_tensor(kv[:, j % 2, :].rearrange("p (d h e) -> p d h e", d=DH, h=H),
                                    k3.unsqueeze(3).to_broadcast([P, DH, H, DH]),
                                    v3.unsqueeze(1).to_broadcast([P, DH, H, DH]), ALU.mult).then_inc(kv_ok, 1)
                    if first and j == 0:
                        norm_queries(0)
                    if more and j == 1:
                        scale_values(b + 1)
                    if more and j == 2:
                        norm_queries(b + 1)

            pool.wait_ge(bvs_ok, 1)
            scale_values(0)
            outer_products(0, True, True)
            with pool.Fori(1, SEQS - 1) as b:
                outer_products(b, False, True)
            outer_products(SEQS - 1, False, False)

            pool.wait_ge(rows_x_out, 16)
            pool.wait_ge(idx_ok, 1)
            pool.sem_inc(o_free, RO)

            units_dram = rows_dram.rearrange("t (i c) -> (t i) c", i=2)

            def gather(s, to, source, index):
                g.indirect_dma_start(rg[:, s % RG, to], None, source[:, :],
                                     bass.IndirectOffsetOnAxis(ap=index[:, s:s + 1], axis=0)).then_inc(gath[s % RG], 16)

            def write(s):
                old = s - UNDER_WAY
                if old >= 0:
                    pool.wait_ge(scat[old % RO], 16 * (old // RO) + 16)
                    pool.sem_inc(o_free, 1)
                pool.wait_ge(o_ok, s + 1)
                g.indirect_dma_start(out_rows[:, :], bass.IndirectOffsetOnAxis(ap=sidx[:, s:s + 1], axis=0),
                                     o[:, s % RO, :], None, bounds_check=TOKENS - 1,
                                     oob_is_err=False).then_inc(scat[s % RO], 16)

            for s in range(EARLY):
                gather(s, slice(0, RS), first_dram, gidx)
            pool.wait_ge(rows_out, 16 * (SEQS + 1))
            for s in range(EARLY):
                pool.wait_ge(gath[s], 16)
                gather(s, slice(RS, RW), units_dram, uidx)
                gather(EARLY + s, slice(0, RW), rows_dram, gidx)
            for s in range(SLOTS):
                write(s)
                if s + RG < SLOTS:
                    gather(s + RG, slice(0, RW), rows_dram, gidx)
            for r in range(RO):
                pool.wait_ge(scat[r], 16 * ((SLOTS - r + RO - 1) // RO))

        @block.scalar
        def _(act):
            a = nc.scalar
            act.dma_start(small[0:E, :], cent).then_inc(small_in, 16)
            act.dma_start(small[E:2 * E, :], ln_g).then_inc(small_in, 16)
            act.dma_start(small[2 * E:3 * E, :], ln_b).then_inc(small_in, 16)
            act.dma_start(small[3 * E:, :], b1.rearrange("e (c p) -> (e c) p", p=P)).then_inc(small_in, 16)
            act.dma_start(wcat[:, CQ:CQ + D], wq).then_inc(w_in, 16)
            act.dma_start(wcat[:, CK:CK + D], wk).then_inc(w_in, 16)
            act.dma_start(wcat[:, CV:CV + D], wv).then_inc(w_in, 16)
            act.dma_start(wcat[:, CB:CB + H], wb).then_inc(w_in, 16)
            act.preload_act_table_set("natural_log_exp_and_others")
            act.wait_ge(small_T, 1)
            a.copy(wcat[:, CA:CA + E], small_ps[:, 0:E])
            a.copy(gb[:, :], small_ps[:, E:3 * E])
            a.copy(b1_sb[:, :, :].rearrange("p e c -> p (e c)"), small_ps[:, 3 * E:]).then_inc(small_ok, 1)

            def rough_scale_1(i):
                n = halves[i]
                act.wait_ge(var1_ok, i + 1)
                a.activation(tmp[:, n], var1[:, n], ACT.Ln).then_inc(sqrt1_ok, 1)
                act.wait_ge(sqrt1_ok, 2 * i + 1)
                a.activation(row[:, n, RSC1], tmp[:, n], ACT.Exp, scale=-0.5).then_inc(sqrt1_ok, 1)
            rough_scale_1(0)

            act.sem_inc(pj_ok, TPS)
            act.wait_ge(scale1_ok, 1)

            def xn_of(b, i, j):
                r = row[:, bass.ds(b * TPS + j, 1), :].rearrange("p o c -> p (o c)")
                a.activation(xs[i][:, j, :], r[:, RX:RX + D], ACT.Identity, bias=r[:, RSH1:RSH1 + 1],
                             scale=r[:, RSC1:RSC1 + 1]).then_inc(xs_act_ok, 1)

            def out_xT(c, j):
                act.wait_ge(xT_ps_ok, c)
                a.copy(xT[:, j % TPS, :], bank[:, 4 + j % 2, 0:P]).then_inc(xT_ok, 1)

            def sequence(b, i, more_xn, more_xT):
                n = b * TPS
                c = ahead(act, *(n + j + 1 for j in range(TPS + 2)))
                if more_xn:
                    before_b = ahead(act, b)[0]
                for j in range(TPS):
                    if j < TPS - 2 or more_xT:
                        out_xT(c[j + 2], j + 2)
                    if j in (0, 1) and more_xn:
                        if j == 0:
                            act.wait_ge(st2_ok, before_b)
                        xn_of(b + 1, 1 - i, 2 + j)
                    act.wait_ge(pj_ps_ok, c[j])
                    a.copy(proj[:, bass.ds(n + j, 1), :], bank[:, j:j + 1, 0:PW]).then_inc(pj_ok, 1)
                    if j == 1 and isinstance(b, int) and b == 0:
                        rough_scale_1(1)
            for b in range(2):
                for j in (2, 3):
                    xn_of(b, b, j)
            out_xT(1, 0)
            out_xT(2, 1)
            sequence(0, 0, False, True)
            act.wait_ge(scale1_ok, 2)
            with act.Fori(0, (SEQS - 2) // 2) as pair:
                for i in (1, 0):
                    sequence(pair * 2 + 2 - i, i, True, True)
            sequence(SEQS - 1, 1, False, False)
            act.wait_ge(ln2_ok, 1)
            a.activation(tmp[:, :], var2[:, :], ACT.Ln).then_inc(r2_ok, 1)
            act.wait_ge(r2_ok, 1)
            a.activation(row[:, :, RSC2], tmp[:, :], ACT.Exp, scale=-0.5).then_inc(r2_ok, 1)
            for i, done in ((1, lnk_ok), (0, lnq_ok)):
                act.wait_ge(ss_ok, 2 - i)
                a.activation(tmp_n[:, :, i, :], ss[:, :, i, :], ACT.Ln).then_inc(done, 1)
                act.wait_ge(done, 1)
                a.activation(rnorm[:, :, i, :], tmp_n[:, :, i, :], ACT.Exp, scale=-0.5).then_inc(done, 1)
                act.wait_ge(done, 2)
                a.activation(tmp_n[:, :, i, :], rnorm[:, :, i, :], ACT.Square).then_inc(done, 1)
            act.wait_ge(logit_ok, 1)
            a.activation(logit, logit, ACT.Sigmoid).then_inc(sig_ok, 1)
            act.wait_ge(mx_ok, 1)
            a.activation(row[:, :, RALPHA], mx[:, :], ACT.Sigmoid).then_inc(alpha_ok, 1)

            act.wait_ge(xT_ps_ok, NT)

            def out_s(n, c, r):
                act.wait_ge(s_ps_ok, c)
                a.copy(row[:, bass.ds(n, 1), RS:RS + D], s_ps.unsqueeze(1)).then_inc(s_ok, 1)

            def out_aT(c, r):
                act.wait_ge(aT_ps_ok, c)
                a.copy(aT[:, r, :], aT_ps).then_inc(aT_ok, 1)

            def stage(n, j):
                a.copy(qk[:, j % 2:j % 2 + 1, :], proj[:, bass.ds(n, 1), CQ:CQ + 2 * D]).then_inc(qk_ok, 1)

            def partition_one_hot(n):
                if not isinstance(n, int) or n:
                    act.wait_ge(ohb_ok, n)
                a.activation(apart, col[:, :], ACT.Square, bias=pb[:, bass.ds(n, 1)], scale=-1.0).then_inc(apart_ok, 1)
                act.wait_ge(apart_ok, n + 1)
                a.activation(ohb[:, bass.ds(n, 1), :].rearrange("p o c -> p (o c)"), apart, ACT.Relu, bias=1.0,
                             scale=-1.0).then_inc(ohb_ok, 1)

            def tiles(b, first, last):
                at = range(0 if first else -1, TPS)
                c = dict(zip(at, ahead(act, *(b * TPS + j for j in at))))
                g = ahead(act, *(b * (TPS - 1) + j for j in range(TPS)))
                for j in range(TPS):
                    n = b * TPS + j
                    if j:
                        act.wait_ge(qT_ps_ok, g[j])
                        a.copy(qT[:, j % 2, :], qT_ps).then_inc(qT_ok, 1)
                    if j >= 2 or not first:
                        out_s(n - 2, c[j - 1], j % 2)
                    if j >= 1 or not first:
                        out_aT(c[j], (j - 1) % 2)
                    if j == 0 and first:
                        act.wait_ge(st_ps_ok, 1)
                    if j < 2 or not last:
                        if j == 2:
                            act.wait_ge(qn_ok, b + 2)
                        stage(n + 2, j)
                    if j == 3 and first:
                        act.wait_ge(valid_ok, 2)
                        a.activation(oha[:, 2, :, :], oha[:, 0, :, :], ACT.Copy, scale=pplus[:, 0:1]).then_inc(oneh_ok, 1)
                    if first and j in (1, 2):
                        act.wait_ge(digits_ok, 1)
                        partition_one_hot(j - 1)
                    elif not first and not last:
                        for i in ((0,), (1, 2), (3, 4), ())[j]:
                            partition_one_hot(2 + (b - 1) * (TPS + 1) + i)
            act.wait_ge(qn_ok, 1)
            stage(0, 0)
            stage(1, 1)
            tiles(0, True, False)
            with act.Fori(1, SEQS - 1) as b:
                tiles(b, False, False)
            tiles(SEQS - 1, False, True)

            act.wait_ge(idx_ok, 1)

            def layernorm_1(s, k, rounds):
                r, n = k % RG, rounds + k // RG
                split = r < EARLY and not (isinstance(n, int) and n == 0)
                act.wait_ge(gath[r], n * 16 + 16 + (16 if split else 0))
                rows = rg[:, r, :]
                a.activation(xn[:, r, :], rows[:, RX:RX + D], ACT.Identity, bias=rows[:, RSH1:RSH1 + 1],
                             scale=rows[:, RSC1:RSC1 + 1]).then_inc(xn_ok, 1)

            def layernorm_2(s, k):
                act.wait_ge(xn_ok, s + 1)
                rows = rg[:, k % RG, :]
                a.activation(xl[:, k % RB, :], xn[:, k % RG, :], ACT.Identity, bias=rows[:, RSH2:RSH2 + 1],
                             scale=rows[:, RSC2:RSC2 + 1]).then_inc(xl_ok, 1)

            def gain_and_shift(s, k, e):
                act.wait_ge(xlT_ps_ok, s + 1)
                a.activation(xlT[:, k % RB, :], xlT_ps, ACT.Identity, bias=gb[:, bass.ds(e + E, 1)],
                             scale=gb[:, bass.ds(e, 1)]).then_inc(xlT_ok, 1)

            for s in range(3):
                layernorm_1(s, s, 0)
                if s < 2:
                    layernorm_2(s, s)
            out_s(NT - 2, NT - 1, 0)
            out_aT(NT, (NT - 1) % 2)
            gain_and_shift(0, 0, act.value_load(sexp_i[0:1, 0:1], min_val=0, max_val=E - 1))
            out_s(NT - 1, NT, 1)

            def step(s, k, rounds, expert_of):
                if real(s - 1):
                    act.wait_ge(b1_ok, s)
                    a.activation(hT[:, (k - 1) % RB, :, :], hT[:, (k - 1) % RB, :, :], ACT.Relu).then_inc(hT_ok, 1)
                if real(s + 2):
                    layernorm_2(s + 2, k + 2)
                if real(s - 2):
                    act.wait_ge(z_ok, s - 1)
                    a.activation(sg[:, (k - 2) % RB, :], y[:, (k - 2) % RB, :], ACT.Sigmoid).then_inc(sg_ok, 1)
                if real(s + 1):
                    gain_and_shift(s + 1, k + 1, expert_of(s + 1, k + 1))
                if real(s + 2):
                    expert_of(s + 2, k + 2)
                if real(s + 3):
                    layernorm_1(s + 3, k + 3, rounds)
            slot_steps(act, step, 0, 2)

        @block.tensor
        def _(pe):
            t = nc.tensor

            def stay_awake(products, spare=7):
                for _ in range(products):
                    t.matmul(bank[:, spare, 0:P], ident[:, :], ident[:, :], start=True, stop=True)
            pe.wait_ge(const_ok, 1)
            stay_awake(8)
            pe.wait_ge(small_in, 64)
            t.transpose(small_ps, small[:, :], ident[0:(3 + FC) * E, 0:(3 + FC) * E]).then_inc(small_T, 1)
            stay_awake(12)
            pe.wait_ge(small_ok, 1)
            pe.wait_ge(w_in, 64)

            def turn_xn(i, j):
                t.transpose(bank[:, 4 + j % 2, 0:P], xs[i][:, j, :], ident[:, :]).then_inc(xT_ps_ok, 1)

            def sequence(b, i, more):
                n = b * TPS
                c = ahead(pe, *(n + j + 1 for j in range(TPS)))
                a2, a3, s2 = ahead(pe, 2 * b + 1, 2 * b + 2, b + 2)
                for j in range(TPS):
                    pe.wait_ge(xT_ok, c[j])
                    if j == 0:
                        pe.wait_ge(xs_act_ok, a2)
                    if j == 1:
                        pe.wait_ge(xs_act_ok, a3)
                    if j < TPS - 2:
                        turn_xn(i, j + 2)
                    elif more:
                        pe.wait_ge(xs_ok, s2)
                        turn_xn(1 - i, j - 2)
                    pe.wait_ge(pj_ok, c[j])
                    t.matmul(bank[:, j, 0:PW], xT[:, j, :], wcat[:, :], start=True, stop=True).then_inc(pj_ps_ok, 1)
            pe.wait_ge(xs_ok, 1)
            turn_xn(0, 0)
            turn_xn(0, 1)
            with pe.Fori(0, SEQS // 2 - 1) as pair:
                for i in range(2):
                    sequence(pair * 2 + i, i, True)
            sequence(SEQS - 2, 0, True)
            sequence(SEQS - 1, 1, False)

            stay_awake(24)
            pe.wait_ge(oh_ok, 1)
            oh2 = oh_all[:, :, :].rearrange("p n e -> p (n e)")
            t.matmul(ranks_ps, before[:, :], oh2, start=True, stop=False)
            for back in range(1, NT + 1):
                last = t.matmul(ranks_ps[:, back * E:], ones[:, :], oh2[:, 0:(NT + 1 - back) * E], start=False,
                                stop=(back == NT))
            last.then_inc(rank_ok, 1)
            stay_awake(20)
            pe.wait_ge(wo_in, 16)

            def turn_output(j, c, g):
                pe.wait_ge(red_ok, c[j + 1])
                if not isinstance(c[j], int) or c[j] > 1:
                    pe.wait_ge(aT_ok, c[j - 1])
                if j % TPS == 0:
                    t.transpose(aT_ps, attn[:, j % 2, :], ident[:, :]).then_inc(aT_ps_ok, 1)
                else:
                    t.matmul(aT_ps, attn[:, j % 2, :], ident[:, :], start=True, stop=False)
                    pe.wait_ge(qT_ok, g[j])
                    pe.wait_ge(st_ok, g[j])
                    t.matmul(aT_ps, state[:, j % TPS - 1, :], qT[:, j % 2, :], start=False, stop=True).then_inc(aT_ps_ok, 1)

            def output_product(j, c):
                pe.wait_ge(aT_ok, c[j])
                if not isinstance(c[j], int) or c[j] > 1:
                    pe.wait_ge(s_ok, c[j - 1])
                t.matmul(s_ps, aT[:, j % 2, :], wo_sb[:, :], start=True, stop=True).then_inc(s_ps_ok, 1)

            def tiles(b, first, last):
                at = range(-2, TPS + 1) if first else range(-3, TPS + 1)
                c = dict(zip(at, ahead(pe, *(b * TPS + j + 1 for j in at))))
                g = {j: s for j, s in zip(range(TPS), ahead(pe, *(b * (TPS - 1) + j for j in range(TPS))))}
                g[-1] = g[0]
                for j in range(TPS):
                    def sums(half):
                        return t.matmul(prefix[:, j % 2, half * BANK:(half + 1) * BANK], tri[:, :],
                                        kv[:, j % 2, half * BANK:(half + 1) * BANK], start=True, stop=True)
                    pe.wait_ge(kv_ok, c[j])
                    if j >= 2 or not first:
                        pe.wait_ge(m_ok, c[j - 2])
                    sums(0)
                    if j:
                        pe.wait_ge(qk_ok, c[j])
                        if j > 1 or not first:
                            pe.wait_ge(qT_ok, g[j - 1])
                        t.transpose(qT_ps, qk[:, j % 2, 0:D], ident[:, :]).then_inc(qT_ps_ok, 1)
                    sums(1).then_inc(pre_ok, 1)
                    if not j:
                        pe.wait_ge(qk_ok, c[j])
                    if j < TPS - 1:
                        if j or not first:
                            pe.wait_ge(st_ok, g[j])
                        t.matmul(st_ps, qk[:, j % 2, D:2 * D],
                                 proj[:, bass.ds(b * TPS + j, 1), CV:CV + D].rearrange("p o c -> p (o c)"), start=(j == 0),
                                 stop=True, skip_group_check=True).then_inc(st_ps_ok, 1)
                    if j == 0 and last:
                        pe.wait_ge(inv_read, 1)
                    if j >= 2 or not first:
                        output_product(j - 2, c)
                    if j or not first:
                        turn_output(j - 1, c, g)
            tiles(0, True, False)
            with pe.Fori(1, SEQS - 1) as b:
                tiles(b, False, False)
            pe.wait_ge(oneh_ok, 3)
            pe.wait_ge(ohb_ok, NT)
            pe.wait_ge(s_ok, (SEQS - 1) * TPS - 2)
            for n in range(NT):
                last = t.matmul(inv_ps, ohb[:, n, :], oha[:, 1:3, n, :], start=(n == 0), stop=(n == NT - 1))
            last.then_inc(inv_ok, 1)
            tiles(SEQS - 1, False, True)
            c = {j: (SEQS - 1) * TPS + j + 1 for j in range(TPS + 1)}
            g = {j: (SEQS - 1) * (TPS - 1) + j for j in range(TPS)}
            pe.wait_ge(m_ok, NT - 1)
            stay_awake(10, 0)
            turn_output(TPS - 1, c, g)
            output_product(TPS - 2, c)

            def transpose_x(s, k):
                pe.wait_ge(xl_ok, s + 1)
                t.transpose(xlT_ps, xl[:, k % RB, :], ident[:, :]).then_inc(xlT_ps_ok, 1)
            transpose_x(0, 0)
            output_product(TPS - 1, c)
            pe.wait_ge(ffn_in, 48)

            def step(s, k, rounds, expert_of):
                if real(s):
                    pe.wait_ge(xlT_ok, s + 1)
                    pe.wait_ge(w1_ok, s + 1)
                    for c in range(FC):
                        last = t.matmul(hT_ps[k % 2][:, c * P:(c + 1) * P], w1s[k % 2][:, c * P:(c + 1) * P],
                                        xlT[:, k % RB, :], start=True, stop=True)
                    last.then_inc(hT_ps_ok, 1)
                    expert_of(s, k)
                if real(s + 1):
                    transpose_x(s + 1, k + 1)
                if real(s - 1):
                    e = expert_of(s - 1, k - 1)
                    if real(s - 3):
                        pe.wait_ge(z_ok, s - 2)
                    t.matmul(y_ps[(k - 1) % 2], ones_row[:, :], b2_sb[:, bass.ds(e, 1), :].rearrange("p o d -> p (o d)"),
                             start=True, stop=False)
                    pe.wait_ge(hT_ok, s)
                    for c in range(FC):
                        last = t.matmul(y_ps[(k - 1) % 2], hT[:, (k - 1) % RB, c, :],
                                        w2_sb[:, bass.ds(e, 1), c, :].rearrange("p o d -> p (o d)"),
                                        start=False, stop=(c == FC - 1))
                    last.then_inc(y_ps_ok, 1)
            slot_steps(pe, step, 1, 0)

        @block.vector
        def _(dve):
            v = nc.vector
            chain = [0]

            def link(ins, meanwhile=None):
                chain[0] += 1
                ins.then_inc(dv, 1)
                if meanwhile:
                    meanwhile()
                dve.wait_ge(dv, chain[0])

            dve.wait_ge(iota_ok, 1)
            v.memset(ones[:, :], 1.0)
            v.memset(ones_row[:, :], 1.0)
            v.memset(row[:, :, RS + D:RW], 0.0)
            v.memset(oh_all[:, NT, :], 0.0)
            for z in pe8:
                v.memset(z[:, :], 0.0)
            link(v.tensor_single_scalar(phead_i[:, :], pidx_i[:, :], 3, ALU.arith_shift_right))
            v.tensor_scalar(tri[:, :], col[:, :], pidx[:, 0:1], None, ALU.is_ge)
            v.tensor_scalar(before[:, :], col[:, :], pidx[:, 0:1], None, ALU.is_gt)
            v.tensor_scalar(ident[:, :], col[:, :], pidx[:, 0:1], None, ALU.is_equal).then_inc(const_ok, 1)
            link(v.tensor_copy(phead[:, :], phead_i[:, :]))
            v.tensor_scalar(same_head[:, :], colhead[:, :, :].rearrange("p h d -> p (h d)"), phead[:, 0:1], None, ALU.is_equal)
            dve.sem_inc(sum_ok, 2)

            def mean_and_variance(st, mean, var, tmp, meanwhile=None):
                v.tensor_tensor(mean, st[:, :, 1], st[:, :, 4], ALU.add)
                v.tensor_tensor(tmp, st[:, :, 1], st[:, :, 4], ALU.subtract)
                link(v.tensor_tensor(var, st[:, :, 2], st[:, :, 5], ALU.add), meanwhile)
                v.tensor_scalar(mean, mean, 0.5, None, ALU.mult)
                v.scalar_tensor_tensor(tmp, tmp, 0.25, tmp, ALU.mult, ALU.mult)
                link(v.tensor_scalar(var, var, 1.0 / D, LN_EPS, ALU.mult, ALU.add), meanwhile)
                return v.tensor_tensor(var, var, tmp, ALU.add)

            def newton(r, a_, t_, meanwhile=None, squared=False):
                if not squared:
                    link(v.tensor_tensor(t_, r, r, ALU.mult), meanwhile)
                link(v.scalar_tensor_tensor(t_, t_, -0.5, a_, ALU.mult, ALU.mult), meanwhile)
                return v.scalar_tensor_tensor(r, t_, 1.5, r, ALU.add, ALU.mult)

            taken = [0]

            def statistics_of_x():
                n = taken[0]
                taken[0] += 1
                if n % (2 * TPS) == 0:
                    dve.wait_ge(x_in[n // (2 * TPS)], 16)
                return v.bn_stats(st1[:, n, :], row[:, n, RX:RX + D])

            def scale_1(i, meanwhile=None):
                n = halves[i]
                mean_and_variance(st1[:, n, :], mean1[:, n], var1[:, n], tmp[:, n], meanwhile).then_inc(var1_ok, 1)
                if meanwhile:
                    meanwhile()
                    meanwhile()
                dve.wait_ge(sqrt1_ok, 2 * i + 2)
                link(newton(row[:, n, RSC1], var1[:, n], tmp[:, n], meanwhile), meanwhile)
                v.scalar_tensor_tensor(row[:, n, RSH1], mean1[:, n], -1.0, row[:, n, RSC1], ALU.mult,
                                       ALU.mult).then_inc(scale1_ok, 1)
                dve.wait_ge(scale1_ok, i + 1)

            for _ in range(NT // 2):
                last = statistics_of_x()
            link(last)
            scale_1(0, statistics_of_x)

            def xn_of(b, i):
                for j in range(2):
                    r = row[:, bass.ds(b * TPS + j, 1), :].rearrange("p o c -> p (o c)")
                    last = v.tensor_scalar(xs[i][:, j, :], r[:, RX:RX + D], r[:, RSC1:RSC1 + 1], r[:, RSH1:RSH1 + 1],
                                           ALU.mult, ALU.add)
                last.then_inc(xs_ok, 1)

            def statistics(b, i, count, count_act):
                dve.wait_ge(xs_ok, count)
                for j in range(TPS):
                    if j == 2:
                        dve.wait_ge(xs_act_ok, count_act)
                    last = v.bn_stats(st2[:, bass.ds(b * TPS + j, 1), :].rearrange("p o c -> p (o c)"), xs[i][:, j, :])
                last.then_inc(st2_ok, 1)

            def squared_norms(b, i, count):
                dve.wait_ge(sq_ok, count)
                v.tensor_reduce(ss[:, bass.ds(b * TPS, TPS), :, :].rearrange("p j a h -> p j (a h)"),
                                sq[i].rearrange("p j (h d) -> p j h d", d=DH), AX.X, ALU.add).then_inc(sum_ok, 1)

            xn_of(0, 0)
            xn_of(1, 1)
            while taken[0] < NT:
                last = statistics_of_x()
            link(last)
            scale_1(1)
            for b in range(2):
                statistics(b, b, b + 1, 2 * b + 2)
            with dve.Fori(0, (SEQS - 2) // 2) as pair:
                for i in range(2):
                    b = pair * 2 + 2 + i
                    turned, b0, b1, a1 = ahead(dve, (b - 1) * TPS, b - 1, b + 1, b * 2 + 2)
                    dve.wait_ge(xT_ps_ok, turned)
                    dve.wait_ge(st2_ok, b0)
                    xn_of(b, i)
                    statistics(b, i, b1, a1)
                    squared_norms(b - 2, i, b0)
            dve.wait_ge(st2_ok, SEQS)
            mean_and_variance(st2, mean2[:, :], var2[:, :], tmp[:, :]).then_inc(ln2_ok, 1)

            def clamp(part):
                return v.tensor_scalar(part, part, NORM_EPS2, None, ALU.max)
            done = (SEQS - 2) * TPS
            dve.wait_ge(sum_ok, SEQS)
            clamp(ss[:, 0:done, :, :].rearrange("p n a h -> p (n a h)"))
            squared_norms(SEQS - 2, 0, SEQS - 1)
            dve.wait_ge(pj_ok, NT + TPS)
            k4 = proj[:, NT - TPS:NT, CK:CK + D]
            link(v.tensor_tensor(sq[1][:, :, D:2 * D], k4, k4, ALU.mult))

            def last_sums(half):
                link(v.tensor_reduce(ss[:, NT - TPS:NT, half, :],
                                     sq[1][:, :, half * D:(half + 1) * D].rearrange("p j (h d) -> p j h d", d=DH), AX.X, ALU.add))
                clamp(ss[:, done:NT, half, :]).then_inc(ss_ok, 1)
            dve.wait_ge(sum_ok, SEQS + 1)
            last_sums(1)
            dve.wait_ge(sq_ok, SEQS)
            last_sums(0)

            aff = proj[:, :, CA:CA + E]

            def over_tiles(ap):
                return ap.unsqueeze(1).to_broadcast([P, NT, E])

            def over_experts(ap):
                return ap.unsqueeze(2).to_broadcast([P, NT, E])
            v.tensor_reduce(mx[:, :], aff, AX.X, ALU.max).then_inc(mx_ok, 1)
            dve.wait_ge(mx_ok, 1)
            link(v.tensor_tensor(eq, aff, over_experts(mx[:, :]), ALU.is_equal))
            link(v.tensor_tensor(eq, eq, over_tiles(rev[:, :]), ALU.mult))
            link(v.tensor_reduce(mw[:, :], eq, AX.X, ALU.max))
            v.tensor_tensor(oh[:, :, :], eq, over_experts(mw[:, :]), ALU.is_equal).then_inc(oh_ok, 1)
            dve.wait_ge(lnk_ok, 3)
            link(newton(rnorm[:, :, 1, :], ss[:, :, 1, :], tmp_n[:, :, 1, :], squared=True))
            dve.wait_ge(r2_ok, 2)
            link(newton(row[:, :, RSC2], var2[:, :], tmp[:, :]))
            v.scalar_tensor_tensor(row[:, :, RSH2], mean2[:, :], -1.0, row[:, :, RSC2], ALU.mult, ALU.mult).then_inc(scalars_ok, 1)
            dve.wait_ge(sig_ok, 1)
            v.tensor_tensor(rnorm[:, :, 1, :], rnorm[:, :, 1, :], logit, ALU.mult).then_inc(bvs_ok, 1)
            dve.wait_ge(rank_ok, 1)
            link(v.tensor_copy(pos[:, 0:E], total_ps))
            link(v.tensor_tensor(cmp, pos[:, 0:E].unsqueeze(2).to_broadcast([P, E, NT]),
                                 steps[:, :].unsqueeze(1).to_broadcast([P, E, NT]), ALU.is_gt))
            link(v.tensor_reduce(pe8[0][:, 4:], cmp, AX.X, ALU.add))
            es = 0
            for shift in (1, 2, 4):
                link(v.tensor_tensor(pe8[1 - es][:, 4:], pe8[es][:, 4:], pe8[es][:, 4 - shift:4 + E - shift], ALU.add))
                es = 1 - es
            link(v.scalar_tensor_tensor(eq, over_tiles(pe8[es][:, 3:3 + E]), float(P),
                                        rank_ps.rearrange("p (n e) -> p n e", e=E), ALU.mult, ALU.add))
            link(v.tensor_tensor(eq, eq, oh[:, :, :], ALU.mult))
            link(v.tensor_reduce(pos[:, :], eq, AX.X, ALU.add))
            link(v.tensor_copy(pos_i[:, :], pos[:, :]))
            v.tensor_single_scalar(pa_i[:, :], pos_i[:, :], 7, ALU.arith_shift_right)
            link(v.tensor_single_scalar(pb_i[:, :], pos_i[:, :], P - 1, ALU.bitwise_and))
            v.tensor_copy(pb[:, :], pb_i[:, :])
            v.tensor_copy(pa[:, :], pa_i[:, :]).then_inc(digits_ok, 1)
            dve.wait_ge(digits_ok, 1)

            def slot_one_hot(quarter):
                n, tiles_ = halves[quarter % 2], [P, NT // 2, SLOTS]
                if quarter < 2:
                    v.tensor_tensor(oha[:, 0, n, :], slotno[:, :].unsqueeze(1).to_broadcast(tiles_),
                                    pa[:, n].unsqueeze(2).to_broadcast(tiles_), ALU.is_equal).then_inc(valid_ok, 1)
                else:
                    dve.wait_ge(valid_ok, quarter - 1)
                    v.tensor_tensor(oha[:, 1, n, :], oha[:, 0, n, :], tileno[:, n].unsqueeze(2).to_broadcast(tiles_),
                                    ALU.mult).then_inc(oneh_ok, 1)

            def slot_experts():
                link(v.tensor_tensor(scmp[:, :, :], slotno[0:1, :].unsqueeze(2).to_broadcast([1, SLOTS, E - 1]),
                                     pe8[es][0:1, 4:4 + E - 1].unsqueeze(1).to_broadcast([1, SLOTS, E - 1]), ALU.is_ge))
                link(v.tensor_reduce(sexp[:, :], scmp[:, :, :], AX.X, ALU.add))
                v.tensor_copy(sexp_i[:, :], sexp[:, :])

            def slot_tokens():
                dve.wait_ge(inv_ok, 1)
                v.tensor_copy(inv[:, :, :].rearrange("p a s -> p (a s)"), inv_ps).then_inc(inv_read, 1)
                dve.wait_ge(inv_read, 1)
                v.scalar_tensor_tensor(tok[:, :], inv[:, 0, :], float(P), inv[:, 1, :], ALU.mult, ALU.add)
                link(v.tensor_scalar(nothing[:, :], inv[:, 1, :], 0.0, None, ALU.is_equal))
                link(v.scalar_tensor_tensor(past[:, :], nothing[:, :], NOWHERE, tok[:, :], ALU.mult, ALU.add))
                v.tensor_scalar(past[:, :], past[:, :], -1.0, None, ALU.add)
                link(v.tensor_tensor(tok[:, :], nothing[:, :], tok[:, :], ALU.add))
                v.tensor_copy(sidx[:, :], past[:, :])
                link(v.tensor_scalar(tok[:, :], tok[:, :], -1.0, None, ALU.add))
                link(v.tensor_copy(gidx[:, :], tok[:, :]))
                link(v.tensor_scalar(tok[:, 0:EARLY], tok[:, 0:EARLY], 2.0, 1.0, ALU.mult, ALU.add))
                v.tensor_copy(uidx[:, :], tok[:, 0:EARLY]).then_inc(idx_ok, 1)

            dve.sem_inc(red_ok, 1)
            slot_one_hot(0)
            slot_one_hot(1)
            slot_experts()
            dve.wait_ge(qn_ok, 1)

            def tiles(b, first):
                counts = ahead(dve, *(b * TPS + j + 1 for j in range(TPS)))
                states = ahead(dve, *(b * (TPS - 1) + j + 1 for j in range(TPS - 1)))
                for j in range(TPS):
                    n = b * TPS + j
                    q3 = proj[:, bass.ds(n, 1), CQ:CQ + D].rearrange("p o (h d) -> p (o d) h", d=DH)
                    if j == 0:
                        dve.wait_ge(qn_ok, b + 1)
                    dve.wait_ge(red_ok, counts[j])
                    dve.wait_ge(pre_ok, counts[j])
                    v.tensor_tensor(m[:, :].rearrange("p (d h e) -> p d h e", d=DH, h=H),
                                    prefix[:, j % 2, :].rearrange("p (d h e) -> p d h e", d=DH, h=H),
                                    q3.unsqueeze(3).to_broadcast([P, DH, H, DH]), ALU.mult).then_inc(m_ok, 1)
                    if j < TPS - 1:
                        dve.wait_ge(st_ps_ok, states[j])
                        v.tensor_tensor(state[:, j, :], st_ps, same_head[:, :], ALU.mult).then_inc(st_ok, 1)
                    dve.wait_ge(m_ok, counts[j])
                    v.tensor_reduce(attn[:, j % 2, :], m[:, :].rearrange("p (d c) -> p c d", d=DH), AX.X,
                                    ALU.add).then_inc(red_ok, 1)
                    if first and j in (1, 2):
                        slot_one_hot(j + 1)
            tiles(0, True)
            with dve.Fori(1, SEQS - 1) as b:
                tiles(b, False)
            slot_tokens()
            tiles(SEQS - 1, False)

            dve.wait_ge(ffn_in, 48)

            def take_w1(s, k, e):
                v.tensor_copy(w1s[k % 2][:, :], w1_sb[:, bass.ds(e, 1), :].rearrange("p o f -> p (o f)")).then_inc(w1_ok, 1)
            take_w1(0, 0, dve.value_load(sexp_i[0:1, 0:1], min_val=0, max_val=E - 1))

            def output_rows(k, count):
                dve.wait_ge(y2_ok, count)
                dve.wait_ge(o_free, count)
                v.tensor_tensor(o[:, k % RO, :], u[:, k % RB, :], rg[:, k % RG, RX:RX + D], ALU.add).then_inc(o_ok, 1)

            def step(s, k, rounds, expert_of):
                done, r, ga = real(s - 2), (k - 2) % RB, (k - 2) % RG
                if real(s + 1):
                    expert_of(s + 1, k + 1)
                if done:
                    dve.wait_ge(y_ps_ok, s - 1)
                    v.scalar_tensor_tensor(y[:, r, :], y_ps[(k - 2) % 2], rg[:, ga, RALPHA:RALPHA + 1], xn[:, ga, :],
                                           ALU.mult, ALU.add).then_inc(z_ok, 1)
                if real(s - 3):
                    output_rows(k - 3, s - 2)
                if real(s + 1):
                    take_w1(s + 1, k + 1, expert_of(s + 1, k + 1))
                if done:
                    dve.wait_ge(z_ok, s - 1)
                    if ga < EARLY:
                        dve.wait_ge(gath[ga], (rounds + (k - 2) // RG) * 16 + 32)
                    v.tensor_tensor(u[:, r, :], y[:, r, :], rg[:, ga, RS:RS + D], ALU.mult).then_inc(u_ok, 1)
                if real(s):
                    e = expert_of(s, k)
                    dve.wait_ge(hT_ps_ok, s + 1)
                    v.tensor_tensor(hT[:, k % RB, :, :], hT_ps[k % 2].rearrange("p (c t) -> p c t", c=FC),
                                    b1_sb[:, bass.ds(e, 1), :].rearrange("p o c -> p (o c)").unsqueeze(2).to_broadcast([P, FC, P]),
                                    ALU.add).then_inc(b1_ok, 1)
                    if real(s + 2):
                        expert_of(s + 2, k + 2)
                if done:
                    dve.wait_ge(sg_ok, s - 1)
                    dve.wait_ge(u_ok, s - 1)
                    v.tensor_tensor(u[:, r, :], u[:, r, :], sg[:, r, :], ALU.mult).then_inc(y2_ok, 1)
            slot_steps(dve, step, 0, 2)
            output_rows(SLOTS - 1, SLOTS)


_INS = ["L0_attn_x", "L0_attn_Wq", "L0_attn_Wk", "L0_attn_Wv", "L0_attn_Wo", "L0_attn_Wb", "L0_attn_bb",
        "L0_ffn_centroids", "L0_ffn_ln_g", "L0_ffn_ln_b", "L0_ffn_w1", "L0_ffn_b1", "L0_ffn_w2", "L0_ffn_b2"]


def kernel(**inputs):
    import numpy as _np
    import concourse.bacc as _bacc
    from concourse.bass_utils import run_bass_kernel_spmd as _run

    nc = _bacc.Bacc("TRN2", target_bir_lowering=False, num_devices=1)
    arrays, args = {}, []
    for name in _INS:
        a = _np.ascontiguousarray(inputs[name])
        arrays[f"in_{name}"] = a
        args.append(nc.dram_tensor(f"in_{name}", a.shape, mybir.dt.from_np(a.dtype), kind="ExternalInput").ap())
    args.append(nc.dram_tensor("out_dram", (SEQS, SEQ, D), F32, kind="ExternalOutput").ap())
    build(nc, *args)
    r = _run(nc, [arrays], core_ids=[0])
    return r.results[0]["out_dram"]
```
